# Optimizing a Trainium2 kernel written in Bass

```python
import numpy as np
import jax
import jax.numpy as jnp

def _softmax(x, axis=-1):
    return jax.nn.softmax(x, axis=axis)

def _gelu(x):
    return jax.nn.gelu(x, approximate=True)

def _silu(x):
    return jax.nn.silu(x)

def _sigmoid(x):
    return jax.nn.sigmoid(x)

def _layernorm(x, axis=-1, eps=1e-05):
    m = jnp.mean(x, axis=axis, keepdims=True)
    v = jnp.var(x, axis=axis, keepdims=True)
    return (x - m) / jnp.sqrt(v + eps)

def _scatter_add(tgt, idx, src, axis=0):
    return tgt.at[idx].add(src)

def _segment_sum(src, seg, n):
    return jax.ops.segment_sum(src, seg, n)
kernel_name = 'mk_flamingo_gated_d1_seqx_r8_f2a7e4'

def setup_inputs(seed: int=0):
    np.random.seed(seed)
    _w = jnp.asarray

    def _rec_inputs():
        import jax
        import jax.numpy as jnp
        _rk = jax.random.key(seed)
        x = 7.22e-05 + 1 * jax.random.normal(jax.random.fold_in(_rk, 1), (16, 128, 256), jnp.float32)
        _lenS = 128 - jax.random.randint(jax.random.fold_in(_rk, 7), (16,), 0, max(1, 128 // 4) + 1, jnp.int32)
        _lenS2 = 128 - jax.random.randint(jax.random.fold_in(_rk, 8), (16,), 0, max(1, 128 // 4) + 1, jnp.int32)
        _ctx_512P = jax.random.normal(jax.random.fold_in(_rk, 11), (16, 16, 64), jnp.float32)
        _ctx_512c = jax.random.dirichlet(jax.random.fold_in(_rk, 511), 0.3 * jnp.ones((16,), jnp.float32), (16, 128))
        _ctx_512t = jnp.einsum('bsk,bkd->bsd', _ctx_512c, _ctx_512P)
        _ctx_512t = _ctx_512t * jax.lax.rsqrt(jnp.mean(jnp.square(_ctx_512t)) + 1e-12) * 0.953939
        ctx_512 = -0.000514642 + 1.00011 * (_ctx_512t + 0.3 * jax.random.normal(jax.random.fold_in(_rk, 611), (16, 128, 64), jnp.float32))
        _g = jax.random.normal(jax.random.fold_in(_rk, 9001), (2, 1), jnp.float32)
        _g = jnp.sign(_g) * jnp.maximum(jnp.abs(_g), 1.0) + (_g == 0) * 1.0
        g_xattn = _g[0]
        g_ffn = _g[1]
        return (x, ctx_512, g_xattn, g_ffn)
    x, ctx_512, g_xattn, g_ffn = _rec_inputs()

    def _L0_xattn_setup():
        import jax, jax.numpy as jnp
        import numpy as np
        B, S, E = (2, 256, 256)
        QH, KVH = (32, 8)
        D = E // QH
        G = QH // KVH
        DROPOUT = 1.0
        key = jax.random.key(seed)
        k1, k2, k3 = jax.random.split(key, 3)
        q = jax.random.normal(k1, (B, S, E), dtype=jnp.float32)
        k = jax.random.normal(k2, (B, S, E // G), dtype=jnp.float32)
        v = jax.random.normal(k3, (B, S, E // G), dtype=jnp.float32)
        return {'q': q, 'k': k, 'v': v}
    _L0_xattn_all = _L0_xattn_setup()
    _L0_xattn_in = {k: v for k, v in _L0_xattn_all.items() if k in ()}
    del _L0_xattn_all

    def _L0_ffn_setup():
        import jax, jax.numpy as jnp
        import numpy as np

        @jax.custom_vjp
        def ste_sign(x):
            return jnp.sign(x)

        def _ste_fwd(x):
            return (jnp.sign(x), None)

        def _ste_bwd(_, g):
            return (g,)
        ste_sign.defvjp(_ste_fwd, _ste_bwd)
        D_MODEL = 256
        D_HIDDEN = 1024
        key = jax.random.key(seed)
        k_x, k_up, k_dn = jax.random.split(key, 3)
        x = jax.random.normal(k_x, (2, 256, D_MODEL), dtype=jnp.float32)
        up_weight = jax.random.normal(k_up, (D_HIDDEN, D_MODEL), dtype=jnp.float32) * 0.02
        down_weight = jax.random.normal(k_dn, (D_MODEL, D_HIDDEN), dtype=jnp.float32) * 0.02
        up_scale = jnp.ones((D_HIDDEN,), dtype=jnp.float32)
        down_scale = jnp.ones((D_MODEL,), dtype=jnp.float32)
        output_scale = jnp.ones((1,), dtype=jnp.float32)
        return {'x': x, 'up_weight': up_weight, 'down_weight': down_weight, 'up_scale': up_scale, 'down_scale': down_scale, 'output_scale': output_scale}
    _L0_ffn_all = _L0_ffn_setup()
    _L0_ffn_in = {k: v for k, v in _L0_ffn_all.items() if k in ('up_weight', 'down_weight', 'up_scale', 'down_scale', 'output_scale')}
    del _L0_ffn_all
    return {'x': x, 'ctx_512': ctx_512, 'g_xattn': g_xattn, 'g_ffn': g_ffn, 'L0_ffn_up_weight': _L0_ffn_in['up_weight'], 'L0_ffn_down_weight': _L0_ffn_in['down_weight'], 'L0_ffn_up_scale': _L0_ffn_in['up_scale'], 'L0_ffn_down_scale': _L0_ffn_in['down_scale'], 'L0_ffn_output_scale': _L0_ffn_in['output_scale']}

def reference(x, ctx_512, g_xattn, g_ffn, L0_ffn_up_weight, L0_ffn_down_weight, L0_ffn_up_scale, L0_ffn_down_scale, L0_ffn_output_scale):
    import jax
    import jax.numpy as jnp

    def _L0_xattn_ref(q, k, v):
        import jax, jax.numpy as jnp
        import numpy as np
        B, S, E = (2, 256, 256)
        QH, KVH = (32, 8)
        D = E // QH
        G = QH // KVH
        DROPOUT = 1.0
        b, s, _ = q.shape
        qh = q.reshape(b, s, KVH, G, D).transpose(0, 2, 3, 1, 4)
        kh = k.reshape(b, s, KVH, D).transpose(0, 2, 1, 3)
        vh = v.reshape(b, s, KVH, D).transpose(0, 2, 1, 3)
        scale = 1.0 / jnp.sqrt(jnp.float32(D))
        scores = jnp.einsum('bkgsd,bktd->bkgst', qh, kh) * scale
        attn = jax.nn.softmax(scores, axis=-1) / DROPOUT
        out = jnp.einsum('bkgst,bktd->bkgsd', attn, vh)
        return out.transpose(0, 3, 1, 2, 4).reshape(b, s, E)

    def _L0_ffn_ref(x, up_weight, down_weight, up_scale, down_scale, output_scale):
        import jax, jax.numpy as jnp
        import numpy as np

        @jax.custom_vjp
        def ste_sign(x):
            return jnp.sign(x)

        def _ste_fwd(x):
            return (jnp.sign(x), None)

        def _ste_bwd(_, g):
            return (g,)
        ste_sign.defvjp(_ste_fwd, _ste_bwd)
        D_MODEL = 256
        D_HIDDEN = 1024
        up_w = ste_sign(up_weight)
        down_w = ste_sign(down_weight)
        hidden = jnp.einsum('bsd,hd->bsh', x, up_w) * up_scale
        hidden = jax.nn.relu(hidden)
        out = jnp.einsum('bsh,dh->bsd', hidden, down_w) * down_scale
        return out * output_scale
    x = x + jnp.tanh(g_xattn[0]) * _L0_xattn_ref(_layernorm(x, axis=-1), ctx_512, ctx_512)
    x = x + jnp.tanh(g_ffn[0]) * _L0_ffn_ref(_layernorm(x, axis=-1), L0_ffn_up_weight, L0_ffn_down_weight, L0_ffn_up_scale, L0_ffn_down_scale, L0_ffn_output_scale)
    return x

_drawn_inputs = setup_inputs


def setup_inputs(seed=0):
    import zlib

    import numpy as np

    out = dict(_drawn_inputs(seed))
    spreads = {'L0_ffn_up_scale': (1.0, 0.2), 'L0_ffn_down_scale': (1.0, 0.2)}
    factors = {}
    for name, (base, spread) in spreads.items():
        noise = np.random.default_rng([zlib.crc32(name.encode()), seed]).standard_normal(out[name].shape)
        drawn = base * np.exp(spread * noise) if base else spread * noise
        out[name] = jnp.asarray(drawn.astype(out[name].dtype))
    for name, factor in factors.items():
        out[name] = (out[name] * factor).astype(out[name].dtype)
    return out
```

```python
import concourse.bass as bass
from concourse import mybir
from contextlib import ExitStack


def flamingo_kernel(nc: bass.Bass, x, ctx_in, g_xattn, g_ffn, up_w, down_w, up_s, down_s, out_s, out):
    fp32, bf16, fp16 = mybir.dt.float32, mybir.dt.bfloat16, mybir.dt.float16
    ALU, ACT, AX = mybir.AluOpType, mybir.ActivationFunctionType, mybir.AxisListType

    B, S, E = x.shape
    KF = ctx_in.shape[2]
    D = 8
    KVH = KF // D
    QH = E // D
    G = QH // KVH
    JP = KVH // 2
    HID = up_w.shape[0]
    HK = HID // 128
    FC = E // 128
    GB = 4
    NG = B // GB
    EPS = 1e-5
    SCALE = float(D) ** -0.5
    SHIFT = float(2 ** 20)
    UP_TARGET = 64.0
    ONE = 3 * D
    NC = KVH
    PIPE = 2

    es = ExitStack()
    with es:
        def sb(name, shape, dt):
            return es.enter_context(nc.sbuf_tensor(name, shape, dt))

        def pb(name, shape, dt):
            return es.enter_context(nc.psum_tensor(name, shape, dt))

        def sem(name):
            return es.enter_context(nc.semaphore(name))

        X = sb("X", [128, B, E], fp32)
        CTX = sb("CTX", [128, B, KF], fp32)
        KP = sb("KP", [128, B * KVH, 2, 32], bf16)
        KR = sb("KR", [128, B * KVH, D], fp32)
        KTA = sb("KTA", [128, B, JP * 128], bf16)
        KTS = [sb(f"KTS{i}", [128, JP, 128], bf16) for i in range(2)]
        KTT = [sb(f"KTT{i}", [128, JP, 128], bf16) for i in range(2)]
        VA = sb("VA", [128, B, KVH * 32], fp32)
        V = [sb(f"V{i}", [128, KVH, 32], fp32) for i in range(2)]
        Q = sb("Q", [128, QH, D], fp32)
        QS = sb("QS", [128, QH, 2, 32], fp16)
        QT = [sb(f"QT{i}", [128, JP, G * 128], fp16) for i in range(2)]
        NM = [sb(f"NM{i}", [128, JP, 2, G], fp32) for i in range(2)]
        MP = sb("MP", [128, 2, 2, 2, G], fp16)
        MT = [sb(f"MT{i}", [32, 128], fp16) for i in range(2)]
        P = [sb(f"P{i}", [128, KVH, G * 128], fp32) for i in range(2)]
        OS = sb("OS", [128, G * 128], fp32)
        RC = [sb(f"RC{i}", [128, G, 4], fp32) for i in range(2)]
        RT = [sb(f"RT{i}", [128, G, 4], fp32) for i in range(2)]
        AO = [sb(f"AO{i}", [128, 2, 4, G, D], fp32) for i in range(2)]
        ST1 = sb("ST1", [128, B, 6], fp32)
        MV1 = sb("MV1", [128, B, 2], fp32)
        VE1 = sb("VE1", [128, B], fp32)
        RS1 = sb("RS1", [128, B], fp32)
        MR1 = sb("MR1", [128, B], fp32)
        NB1 = sb("NB1", [128, B], fp32)
        HALF = sb("HALF", [128, B], fp32)
        IDF = sb("IDF", [128, 128], fp32)
        IDH = sb("IDH", [128, 128], fp16)
        IDB = sb("IDB", [128, 128], bf16)
        GX = sb("GX", [128, 1], fp32)
        TX = sb("TX", [128, 1], fp32)
        GF = sb("GF", [128, 1], fp32)
        TF = sb("TF", [128, 1], fp32)
        OSC = sb("OSC", [128, 1], fp32)
        DS = sb("DS", [128, E], fp32)
        CS = sb("CS", [128, E], fp32)
        US = sb("US", [128, HK], fp32)
        UN = sb("UN", [128, HK], fp32)
        um = sb("um", [128, 1], fp32)
        uma = sb("uma", [128, 1], fp32)
        umg = sb("umg", [128, 1], fp32)
        umr = sb("umr", [128, 1], fp32)
        fac = sb("fac", [128, 3], fp32)
        UW = sb("UW", [128, HK, E], fp32)
        DW = sb("DW", [128, FC, HID], fp32)
        NEG = sb("NEG", [128, HK * E], fp16)
        SU = sb("SU", [128, HK, E], fp16)
        SD = sb("SD", [128, FC, HID], fp16)
        UT = sb("UT", [128, FC, HID], fp16)
        DT = sb("DT", [128, HK, E], fp16)
        ST2 = sb("ST2", [128, GB, 6], fp32)
        MV2 = sb("MV2", [128, GB, 2], fp32)
        VE2 = sb("VE2", [128, GB], fp32)
        RS2 = sb("RS2", [128, GB], fp32)
        XN = sb("XN", [128, GB, E], fp32)
        XH = sb("XH", [128, 2, GB, E], fp16)
        XT = sb("XT", [128, 2, FC, GB * 128], fp16)
        HF = [sb(f"HF{i}", [128, 512], fp32) for i in range(2)]
        HP = [sb(f"HP{i}", [128, 2, 512], fp16) for i in range(4)]
        YS = sb("YS", [128, GB, E], fp32)

        PS_ = [pb(f"PS{i}", [128, 512], fp32) for i in range(2)]
        PT_ = [pb(f"PT{i}", [128, 512], fp32) for i in range(2)]
        PQ = pb("PQ", [128, 512], fp32)
        PM = pb("PM", [128, 512], fp32)
        PO = pb("PO", [128, 512], fp32)
        PX = pb("PX", [128, 512], fp32)
        PQh, PQb, PMh = PQ[:, :].bitcast(fp16), PQ[:, :].bitcast(bf16), PM[:, :].bitcast(fp16)
        UPB = [PS_[0], PS_[1], PM]
        YB = [PT_[0], PT_[1], PO, PX]

        ld_ctx = sem("ld_ctx")
        ld_x = [sem(f"ld_x{i}") for i in range(NG)]
        ld_small = sem("ld_small")
        ld_w = sem("ld_w")
        ident = sem("ident")
        zeroed = sem("zeroed")
        k_hi, k_r1, k_mid, k_r2, k_lo = (sem(n) for n in ("k_hi", "k_r1", "k_mid", "k_r2", "k_lo"))
        v_ready = sem("v_ready")
        k_tr, k_ev = sem("k_tr"), sem("k_ev")
        st_ready, mv_ready, ve_ready, rs_ready, mr_ready, nb_ready = (
            sem(n) for n in ("st_ready", "mv_ready", "ve_ready", "rs_ready", "mr_ready", "nb_ready"))
        tx_ready = sem("tx_ready")
        q_ready, hi_ready, lo_ready = sem("q_ready"), sem("hi_ready"), sem("lo_ready")
        qtr_done, qt_ready = sem("qtr_done"), sem("qt_ready")
        kts_ld = [sem(f"kts_ld{i}") for i in range(2)]
        ktt_ld = [sem(f"ktt_ld{i}") for i in range(2)]
        v_ld = [sem(f"v_ld{i}") for i in range(2)]
        s_done, max_done = sem("s_done"), sem("max_done")
        mh_ready, mp_ready, mtr_done, mt_ready = sem("mh_ready"), sem("mp_ready"), sem("mtr_done"), sem("mt_ready")
        m_ld = [sem(f"m_ld{i}") for i in range(2)]
        t_done, exp_done = sem("t_done"), sem("exp_done")
        pv_done, os_ready, otr_done = sem("pv_done"), sem("os_ready"), sem("otr_done")
        rc_ready, ao_ready, x1_ready = sem("rc_ready"), sem("ao_ready"), sem("x1_ready")
        neg_done, sign_done = sem("neg_done"), sem("sign_done")
        wtr_done, wt_ready = sem("wtr_done"), sem("wt_ready")
        um_ready, uma_ready, us_step, un_ready, cs_ready = (
            sem(n) for n in ("um_ready", "uma_ready", "us_step", "un_ready", "cs_ready"))
        st2_ready, mv2_ready, ve2_ready, rs2_ready, xn_ready, xh_ready, xl_ready = (
            sem(n) for n in ("st2_ready", "mv2_ready", "ve2_ready", "rs2_ready", "xn_ready", "xh_ready", "xl_ready"))
        xtr_done, xt_ready = sem("xtr_done"), sem("xt_ready")
        up_done, h_ready, hh_ready, hl_ready, down_k, y_done = (
            sem(n) for n in ("up_done", "h_ready", "hh_ready", "hl_ready", "down_k", "y_done"))
        ys_ready, y_ready, stored = sem("ys_ready"), sem("y_ready"), sem("stored")

        block = es.enter_context(nc.Block())

        HEAD, TAIL = (-2, -1, 0, 1), (B - 2, B - 1, B)
        LOOP = (2, B - 2)

        def steps(engine, step):
            for t in HEAD:
                step(t, t % 2, t)
            with engine.Fori(0, (LOOP[1] - LOOP[0]) // PIPE) as i:
                for u in range(PIPE):
                    step(i * PIPE + LOOP[0] + u, (LOOP[0] + u) % 2, None)
            for t in TAIL:
                step(t, t % 2, t)

        def has(t, d):
            return t is None or 0 <= t + d < B

        def turn(t, par, d):
            odd = (par + d) % 2
            return (t + d - odd) // 2 + 1 if isinstance(t, int) else (t + (d - odd)) // 2 + 1

        @block.sync
        def _(sp):
            sp.dma_start(CTX[:, :, :], ctx_in.rearrange("b s f -> s b f")).then_inc(ld_ctx, 16)
            for n in range(NG):
                sp.dma_start(X[:, n * GB:(n + 1) * GB, :],
                             x[n * GB:(n + 1) * GB, :, :].rearrange("b s f -> s b f")).then_inc(ld_x[n], 16)
            sp.dma_start(GX[:, :], g_xattn[None, :].to_broadcast([128, 1])).then_inc(ld_small, 16)
            sp.dma_start(GF[:, :], g_ffn[None, :].to_broadcast([128, 1])).then_inc(ld_small, 16)
            sp.dma_start(OSC[:, :], out_s[None, :].to_broadcast([128, 1])).then_inc(ld_small, 16)
            sp.dma_start(DS[:, :], down_s[None, :].to_broadcast([128, E])).then_inc(ld_small, 16)
            sp.dma_start(US[:, :], up_s.rearrange("(k p) -> p k", p=128),
                         allow_slow_non_contiguous=True).then_inc(ld_small, 16)
            sp.dma_start(UW[:, :, :], up_w.rearrange("(k p) f -> p k f", p=128)).then_inc(ld_w, 16)
            sp.dma_start(DW[:, :, :], down_w.rearrange("(c p) h -> p c h", p=128)).then_inc(ld_w, 16)

            def shift_rows(b, hf, par):
                sp.dma_start(QT[par][ONE:128:32, 2 * hf:2 * hf + 2, :], MT[hf][:, :]).then_inc(m_ld[hf], 16)

            def step(t, par, tt):
                nxt = 1 - par
                if has(tt, 2):
                    if tt is None or tt >= 0:
                        sp.wait_ge(s_done, NC * (t + 1))
                    if tt == -2:
                        sp.wait_ge(k_ev, B // 2)
                    sp.dma_start(KTS[par][:, :, :], KTA[:, bass.ds(t + 2, 1), :].rearrange(
                        "p o (j t) -> p (o j) t", j=JP)).then_inc(kts_ld[par], 16)
                if has(tt, 1):
                    if tt is None or tt >= 1:
                        sp.wait_ge(t_done, NC * t)
                    sp.dma_start(KTT[nxt][:, :, :], KTA[:, bass.ds(t + 1, 1), :].rearrange(
                        "p o (j t) -> p (o j) t", j=JP)).then_inc(ktt_ld[nxt], 16)
                if has(tt, 0):
                    sp.wait_ge(mt_ready, 2 * t + 2)
                    shift_rows(t, 1, par)
                if has(tt, 1):
                    if tt == -1:
                        sp.wait_ge(v_ready, 1)
                    if tt is None or tt >= 1:
                        sp.wait_ge(pv_done, 2 * t)
                    sp.dma_start(V[nxt][:, :, :], VA[:, bass.ds(t + 1, 1), :].rearrange(
                        "p o (j c) -> p (o j) c", j=KVH)).then_inc(v_ld[nxt], 16)
                    sp.wait_ge(mt_ready, 2 * (t + 1) + 1)
                    shift_rows(t + 1, 0, nxt)
            steps(sp, step)

            for n in range(NG):
                sp.wait_ge(y_ready, GB * (n + 1))
                sp.dma_start(out[n * GB:(n + 1) * GB, :, :].rearrange("b s f -> s b f"),
                             X[:, n * GB:(n + 1) * GB, :]).then_inc(stored, 16)
            sp.wait_ge(stored, 16 * NG)

        @block.gpsimd
        def _(pool):
            nc.gpsimd.memset(HALF[:, :], -0.5)
            nc.gpsimd.memset(IDF[:, :], 0.0).then_inc(zeroed, 1)
            pool.wait_ge(zeroed, 1)
            nc.gpsimd.affine_select(out=IDF[:, :], in_=IDF[:, :], compare_op=ALU.not_equal, fill=1.0, base=0,
                                    pattern=[[-1, 128]], channel_multiplier=1).then_inc(ident, 1)
            for n in range(NG):
                r = slice(n * GB, (n + 1) * GB)
                pool.wait_ge(ve_ready, n + 1)
                nc.gpsimd.tensor_tensor(RS1[:, r], VE1[:, r], HALF[:, r], ALU.pow).then_inc(rs_ready, 1)
                if n == 0:
                    nc.gpsimd.memset(VA[:, :, :], 0.0).then_inc(zeroed, 1)
                    pool.wait_ge(zeroed, 2)
                    pool.wait_ge(ld_ctx, 16)
                    va = VA[:, :, :].rearrange("p b (j c) -> p (b j) c", c=32)
                    nc.gpsimd.tensor_copy(va[:, :, 0:D], CTX[:, :, :].rearrange("p b (j d) -> p (b j) d", d=D))
                    nc.gpsimd.memset(va[:, :, D:D + 1], 1.0).then_inc(v_ready, 1)

            pool.wait_ge(ld_w, 32)
            for n, (src, dst) in enumerate(((UW[:, :, :].rearrange("p a b -> p (a b)"),
                                             SU[:, :, :].rearrange("p a b -> p (a b)")),
                                            (DW[:, :, :].rearrange("p a b -> p (a b)"),
                                             SD[:, :, :].rearrange("p a b -> p (a b)")))):
                if n:
                    pool.wait_ge(sign_done, n)
                nc.gpsimd.tensor_scalar(NEG[:, :], src, 0.0, None, ALU.is_lt).then_inc(neg_done, 1)
                pool.wait_ge(neg_done, 2 * n + 1)
                nc.gpsimd.tensor_scalar(src, src, 0.0, None, ALU.is_gt).then_inc(neg_done, 1)
                pool.wait_ge(neg_done, 2 * n + 2)
                nc.gpsimd.tensor_tensor(dst, src, NEG[:, :], ALU.subtract).then_inc(sign_done, 1)

            pool.wait_ge(um_ready, 1)
            nc.gpsimd.partition_all_reduce(uma[:, :], um[:, :], 128, bass.bass_isa.ReduceOp.max).then_inc(uma_ready, 1)

            def step(t, par, tt):
                if has(tt, -1):
                    pool.wait_ge(ao_ready, 2 * t)
                    xb = X[:, bass.ds(t - 1, 1), :].rearrange("p o f -> p (o f)")
                    nc.gpsimd.tensor_tensor(xb, xb, AO[1 - par][:, :, :, :, :].rearrange("p h c g d -> p (h c g d)"),
                                            ALU.add).then_inc(x1_ready, 1)
            steps(pool, step)

            for n in range(NG):
                pool.wait_ge(ve2_ready, n + 1)
                nc.gpsimd.tensor_tensor(RS2[:, :], VE2[:, :], HALF[:, 0:GB], ALU.pow).then_inc(rs2_ready, 1)

        @block.scalar
        def _(act):
            act.wait_ge(ld_small, 80)
            nc.scalar.activation(TX[:, :], GX[:, :], ACT.Tanh).then_inc(tx_ready, 1)
            nc.scalar.activation(TF[:, :], GF[:, :], ACT.Tanh).then_inc(tx_ready, 1)
            act.wait_ge(k_r1, 1)
            nc.scalar.copy(KP[:, :, 0, D:2 * D], KR[:, :, :]).then_inc(k_mid, 1)

            def step(t, par, tt):
                for c in range(NC):
                    if has(tt, 0):
                        act.wait_ge(t_done, NC * t + c + 1)
                        if tt is None or tt >= 2:
                            if c % 4 == 0:
                                act.wait_ge(pv_done, 2 * (t - 2) + c // 4 + 1)
                        nc.scalar.activation(P[par][:, c, :], PT_[c % 2][:, :], ACT.Exp,
                                             scale=SCALE).then_inc(exp_done, 1)
                    if c == 0 and has(tt, 2):
                        if tt == -2:
                            act.wait_ge(nb_ready, NG)
                        else:
                            act.wait_ge(lo_ready, t + 2)
                        for side in range(2):
                            nc.scalar.activation(
                                Q[:, :, :].rearrange("p (j g s) d -> p j g s d", j=JP, s=2)[:, :, :, side, :],
                                X[:, bass.ds(t + 2, 1), :].rearrange(
                                    "p o (j s g d) -> p (o j) s g d", j=JP, s=2, d=D)[:, :, side, :, :],
                                ACT.Identity, bias=NB1[:, bass.ds(t + 2, 1)],
                                scale=RS1[:, bass.ds(t + 2, 1)]).then_inc(q_ready, 1)
                    if c == 1 and has(tt, 2):
                        act.wait_ge(q_ready, 2 * (t + 3))
                        if tt != -2:
                            act.wait_ge(qtr_done, 2 * (t + 2))
                        nc.scalar.copy(QS[:, :, 0, 0:ONE].rearrange("p h (r d) -> p h r d", d=D),
                                       Q[:, :, :].rearrange("p h (o d) -> p h o d", o=1).to_broadcast(
                                           [128, QH, 3, D])).then_inc(hi_ready, 1)
                    if c == 2 and has(tt, -1):
                        act.wait_ge(pv_done, 2 * t)
                        act.wait_ge(otr_done, 2 * t - 1)
                        nc.scalar.copy(OS[:, :], PO[:, :]).then_inc(os_ready, 1)
                    if c == 5 and has(tt, 0):
                        act.wait_ge(pv_done, 2 * t + 1)
                        if tt is None or tt >= 1:
                            act.wait_ge(otr_done, 2 * t)
                        nc.scalar.copy(OS[:, :], PO[:, :]).then_inc(os_ready, 1)
            steps(act, step)

            def high(n):
                act.wait_ge(xn_ready, n + 1)
                if n:
                    act.wait_ge(xtr_done, 2 * n)
                nc.scalar.copy(XH[:, 0, :, :], XN[:, :, :]).then_inc(xh_ready, 1)

            high(0)
            act.wait_ge(un_ready, 1)
            for n in range(NG):
                for k in range(HK):
                    m = n * HK + k
                    act.wait_ge(up_done, m + 1)
                    if m >= 2:
                        act.wait_ge(hl_ready, m - 1)
                    nc.scalar.activation(HF[m % 2][:, :], UPB[m % 3][:, :], ACT.Relu,
                                         scale=UN[:, k:k + 1]).then_inc(h_ready, 1)
                    if m >= 4:
                        nd, kd = divmod(m - 4, HK)
                        if kd < HK - 1:
                            act.wait_ge(down_k, nd * (HK - 1) + kd + 1)
                        else:
                            act.wait_ge(y_done, (nd + 1) * GB)
                    nc.scalar.activation(HP[m % 4][:, 0, :], UPB[m % 3][:, :], ACT.Relu,
                                         scale=UN[:, k:k + 1]).then_inc(hh_ready, 1)
                    if k == 4 and n + 1 < NG:
                        high(n + 1)

        @block.vector
        def _(dve):
            CX = CTX[:, :, :].rearrange("p b (j d) -> p (b j) d", d=D)
            nc.vector.memset(KP[:, :, 0, ONE + 1:32], 0.0)
            nc.vector.memset(KP[:, :, 0, ONE:ONE + 1], SHIFT)
            nc.vector.memset(QS[:, :, :, ONE:32], 0.0)
            dve.wait_ge(ld_ctx, 16)
            nc.vector.tensor_copy(KP[:, :, 0, 0:D], CX).then_inc(k_hi, 1)
            dve.wait_ge(k_hi, 1)
            nc.vector.tensor_tensor(KR[:, :, :], CX, KP[:, :, 0, 0:D], ALU.subtract).then_inc(k_r1, 1)
            dve.wait_ge(ident, 1)
            nc.vector.tensor_copy(IDH[:, :], IDF[:, :])
            nc.vector.tensor_copy(IDB[:, :], IDF[:, :]).then_inc(ident, 1)
            dve.wait_ge(k_mid, 1)
            nc.vector.tensor_tensor(KP[:, :, 0, 2 * D:3 * D], KR[:, :, :], KP[:, :, 0, D:2 * D],
                                    ALU.subtract).then_inc(k_lo, 1)
            dve.wait_ge(k_lo, 1)
            nc.vector.tensor_copy(KP[:, :, 1, :], KP[:, :, 0, :]).then_inc(k_lo, 1)
            for n in range(NG):
                r = slice(n * GB, (n + 1) * GB)
                dve.wait_ge(ld_x[n], 16)
                for b in range(n * GB, (n + 1) * GB):
                    nc.vector.bn_stats(ST1[:, b, :], X[:, b, :]).then_inc(st_ready, 1)
                for b in range(n * GB, (n + 1) * GB):
                    dve.wait_ge(st_ready, b + 1)
                    nc.vector.bn_aggr(MV1[:, b, :], ST1[:, b, :]).then_inc(mv_ready, 1)
                dve.wait_ge(mv_ready, (n + 1) * GB)
                nc.vector.tensor_scalar(VE1[:, r], MV1[:, r, 1], EPS, None, ALU.add).then_inc(ve_ready, 1)
                for i in range(2 * n, 2 * n + 2):
                    dve.wait_ge(k_tr, i + 1)
                    nc.vector.tensor_copy(KTA[:, 2 * i:2 * i + 2, :].rearrange("p b n -> p (b n)"),
                                          PQb[:, 0:1024]).then_inc(k_ev, 1)
            for n in range(NG):
                r = slice(n * GB, (n + 1) * GB)
                dve.wait_ge(rs_ready, n + 1)
                nc.vector.scalar_tensor_tensor(NB1[:, r], MV1[:, r, 0], -1.0, RS1[:, r], ALU.mult,
                                               ALU.mult).then_inc(nb_ready, 1)
            dve.wait_ge(ld_small, 80)
            nc.vector.tensor_reduce(um[:, :], US[:, :], AX.X, ALU.max, apply_absolute_value=True).then_inc(um_ready, 1)

            def maxima(t, c, par):
                dve.wait_ge(s_done, NC * t + c + 1)
                nc.vector.tensor_reduce(NM[par][:, c // 2, c % 2, :], PS_[c % 2][:, :].rearrange(
                    "p (g t) -> p g t", g=G), AX.X, ALU.max, negate=True).then_inc(max_done, 1)

            def shift_parts(b, hf, par, first):
                nm = NM[par][:, 2 * hf:2 * hf + 2, :, :].rearrange("p a b g -> p b a g")
                dve.wait_ge(max_done, NC * b + 4 * hf + 4)
                if not first:
                    dve.wait_ge(mtr_done, 2 * b + hf)
                for side in range(2):
                    last = nc.vector.tensor_scalar(MP[:, side, 0, :, :], nm[:, side, :, :], 1.0 / SHIFT, None,
                                                   ALU.mult)
                last.then_inc(mh_ready, 1)
                dve.wait_ge(mh_ready, 2 * b + hf + 1)
                for side in range(2):
                    last = nc.vector.scalar_tensor_tensor(MP[:, side, 1, :, :], nm[:, side, :, :], 1.0 / SHIFT,
                                                          MP[:, side, 0, :, :], ALU.mult, ALU.subtract)
                last.then_inc(mp_ready, 1)

            def shift_out(b, hf, first):
                dve.wait_ge(mtr_done, 2 * b + hf + 1)
                if not first:
                    dve.wait_ge(m_ld[hf], 16 * b)
                nc.vector.tensor_copy(MT[hf][:, :], PMh[0:32, 0:128]).then_inc(mt_ready, 1)

            def stacked_out(b, r, par, old):
                dve.wait_ge(qtr_done, 2 * b + r + 1)
                if old:
                    dve.wait_ge(t_done, NC * (b - 2) + 4 * r + 4)
                nc.vector.tensor_copy(QT[par][:, 2 * r:2 * r + 2, :].rearrange("p a n -> p (a n)"),
                                      PQh[:, 0:1024]).then_inc(qt_ready, 1)

            def normalise(b, hf, par, old):
                o = PX[:, :].rearrange("p (g c r) -> p g c r", g=G, c=4)
                dve.wait_ge(otr_done, 2 * b + hf + 1)
                nc.vector.reciprocal(RC[hf][:, :, :], o[:, :, :, D]).then_inc(rc_ready, 1)
                dve.wait_ge(rc_ready, 4 * b + 2 * hf + 1)
                nc.vector.tensor_scalar(RT[hf][:, :, :], RC[hf][:, :, :], TX[:, 0:1], None, ALU.mult).then_inc(rc_ready, 1)
                dve.wait_ge(rc_ready, 4 * b + 2 * hf + 2)
                if old:
                    dve.wait_ge(x1_ready, b - 1)
                nc.vector.tensor_tensor(
                    AO[par][:, hf, :, :, :].rearrange("p c g d -> p g c d"), o[:, :, :, 0:D],
                    RT[hf][:, :, :].rearrange("p g (c o) -> p g c o", o=1).to_broadcast([128, G, 4, D]),
                    ALU.mult).then_inc(ao_ready, 1)

            def step(t, par, tt):
                nxt = 1 - par
                for c in range(NC):
                    if has(tt, 1):
                        if c == 2:
                            stacked_out(t + 1, 1, nxt, tt is None or tt >= 1)
                        maxima(t + 1, c, nxt)
                    if c == 1:
                        if has(tt, 0):
                            shift_out(t, 1, tt == 0)
                    if c == 3 and has(tt, 1):
                        shift_parts(t + 1, 0, nxt, tt == -1)
                    if c == 4 and has(tt, -1):
                        normalise(t - 1, 1, nxt, False)
                    if c == 3 and has(tt, 2):
                        dve.wait_ge(hi_ready, t + 3)
                        nc.vector.tensor_tensor(
                            QS[:, :, 1, 0:ONE].rearrange("p h (r d) -> p h r d", d=D),
                            Q[:, :, :].rearrange("p h (o d) -> p h o d", o=1).to_broadcast([128, QH, 3, D]),
                            QS[:, :, 0, 0:ONE].rearrange("p h (r d) -> p h r d", d=D),
                            ALU.subtract).then_inc(lo_ready, 1)
                    if c == 5 and has(tt, 1):
                        shift_out(t + 1, 0, tt == -1)
                    if c == 6 and has(tt, 2):
                        stacked_out(t + 2, 0, par, tt is None or tt >= 0)
                    if c == 7:
                        if has(tt, 1):
                            shift_parts(t + 1, 1, nxt, False)
                        if has(tt, 0):
                            if tt == 0:
                                dve.wait_ge(tx_ready, 2)
                            normalise(t, 0, par, tt is None or tt >= 2)
            steps(dve, step)

            for i in range(4):
                dve.wait_ge(wtr_done, i + 1)
                dst = UT[:, i, :] if i < FC else DT[:, 4 * (i - FC):4 * (i - FC) + 4, :].rearrange("p k n -> p (k n)")
                nc.vector.tensor_copy(dst, PQh[:, 0:1024]).then_inc(wt_ready, 1)
            dve.wait_ge(uma_ready, 1)
            nc.vector.tensor_scalar(umg[:, :], uma[:, :], 1e-30, None, ALU.max).then_inc(us_step, 1)
            dve.wait_ge(us_step, 1)
            nc.vector.reciprocal(umr[:, :], umg[:, :]).then_inc(us_step, 1)
            dve.wait_ge(us_step, 2)
            nc.vector.tensor_scalar(UN[:, :], US[:, :], umr[:, 0:1], UP_TARGET, ALU.mult, ALU.mult).then_inc(un_ready, 1)
            nc.vector.tensor_scalar(fac[:, 0:1], umg[:, :], TF[:, 0:1], 1.0 / UP_TARGET, ALU.mult,
                                    ALU.mult).then_inc(us_step, 1)
            dve.wait_ge(us_step, 3)
            nc.vector.tensor_scalar(CS[:, :], DS[:, :], OSC[:, 0:1], fac[:, 0:1], ALU.mult, ALU.mult).then_inc(cs_ready, 1)

            def norm_group(n):
                for i in range(GB):
                    b = n * GB + i
                    dve.wait_ge(x1_ready, b + 1)
                    nc.vector.bn_stats(ST2[:, i, :], X[:, b, :]).then_inc(st2_ready, 1)
                for i in range(GB):
                    dve.wait_ge(st2_ready, n * GB + i + 1)
                    nc.vector.bn_aggr(MV2[:, i, :], ST2[:, i, :]).then_inc(mv2_ready, 1)
                dve.wait_ge(mv2_ready, (n + 1) * GB)
                nc.vector.tensor_scalar(VE2[:, :], MV2[:, :, 1], EPS, None, ALU.add).then_inc(ve2_ready, 1)

            def apply_group(n):
                dve.wait_ge(rs2_ready, n + 1)
                for i in range(GB):
                    last = nc.vector.tensor_scalar(XN[:, i, :], X[:, n * GB + i, :], MV2[:, i, 0:1], RS2[:, i:i + 1],
                                                   ALU.subtract, ALU.mult)
                last.then_inc(xn_ready, 1)

            def low_group(n):
                dve.wait_ge(xh_ready, n + 1)
                nc.vector.tensor_tensor(XH[:, 1, :, :], XN[:, :, :], XH[:, 0, :, :], ALU.subtract).then_inc(xl_ready, 1)

            def tokens_out(n):
                for p in range(2):
                    dve.wait_ge(xtr_done, 2 * n + p + 1)
                    if n and p == 0:
                        dve.wait_ge(up_done, HK * n)
                    nc.vector.tensor_copy(XT[:, p, :, :].rearrange("p c n -> p (c n)"),
                                          PQh[:, 0:1024]).then_inc(xt_ready, 1)

            norm_group(0)
            apply_group(0)
            low_group(0)
            tokens_out(0)
            for n in range(NG):
                for k in range(HK):
                    m = n * HK + k
                    dve.wait_ge(hh_ready, m + 1)
                    nc.vector.tensor_tensor(HP[m % 4][:, 1, :], HF[m % 2][:, :], HP[m % 4][:, 0, :],
                                            ALU.subtract).then_inc(hl_ready, 1)
                    if n + 1 < NG:
                        if k == 1:
                            norm_group(n + 1)
                        if k == 3:
                            apply_group(n + 1)
                        if k == 5:
                            low_group(n + 1)
                if n + 1 < NG:
                    tokens_out(n + 1)
                if n == 0:
                    dve.wait_ge(cs_ready, 1)
                for i in range(GB):
                    dve.wait_ge(y_done, n * GB + i + 1)
                    nc.vector.tensor_tensor(YS[:, i, :], YB[i][:, 0:E], CS[:, :], ALU.mult).then_inc(ys_ready, 1)
                for i in range(GB):
                    dve.wait_ge(ys_ready, n * GB + i + 1)
                    nc.vector.tensor_tensor(X[:, n * GB + i, :], X[:, n * GB + i, :], YS[:, i, :],
                                            ALU.add).then_inc(y_ready, 1)

        @block.tensor
        def _(pe):
            pe.wait_ge(ident, 2)
            pe.wait_ge(k_lo, 2)
            for i in range(B // 2):
                if i:
                    pe.wait_ge(k_ev, i)
                for a in range(2 * JP):
                    g0 = (2 * i * KVH) + 2 * a
                    w = KP[:, g0:g0 + 2, :, :].rearrange("p j o c -> p (j o c)")
                    last = nc.tensor.transpose(PQb[:, a * 128:(a + 1) * 128], w, IDB[:, :])
                last.then_inc(k_tr, 1)

            def stack(b, r):
                pe.wait_ge(lo_ready, b + 1)
                for a in range(2):
                    for g in range(G):
                        h0 = 2 * ((2 * r + a) * G + g)
                        last = nc.tensor.transpose(
                            PQh[:, (a * G + g) * 128:(a * G + g + 1) * 128],
                            QS[:, h0:h0 + 2, :, :].rearrange("p h c r -> p (h c r)"), IDH[:, :])
                last.then_inc(qtr_done, 1)

            def scores(b, c, par):
                rows = slice(64 * (c % 2), 64 * (c % 2) + 64)
                for g in range(G):
                    last = nc.tensor.matmul(PS_[c % 2][:, g * 128:(g + 1) * 128],
                                            QT[par][rows, c // 2, g * 128:(g + 1) * 128],
                                            KTS[par][rows, c // 2, :], start=True, stop=True)
                last.then_inc(s_done, 1)

            def shifted(b, c, par):
                rows = slice(64 * (c % 2), 64 * (c % 2) + 64)
                nc.tensor.matmul(PT_[c % 2][:, :], KTT[par][rows, c // 2, :], QT[par][rows, c // 2, :],
                                 start=True, stop=True).then_inc(t_done, 1)

            def sums(b, hf, par):
                for c in range(4):
                    last = nc.tensor.matmul(PO[32 * c:32 * c + 32, :], V[par][:, 4 * hf + c, :],
                                            P[par][:, 4 * hf + c, :], start=True, stop=True)
                last.then_inc(pv_done, 1)

            def queries_back(b, hf):
                pe.wait_ge(os_ready, 2 * b + hf + 1)
                for g in range(G):
                    last = nc.tensor.transpose(PX[:, g * 128:(g + 1) * 128], OS[:, g * 128:(g + 1) * 128], IDF[:, :])
                last.then_inc(otr_done, 1)

            def shift_back(b, hf):
                pe.wait_ge(mp_ready, 2 * b + hf + 1)
                nc.tensor.transpose(PMh[0:32, 0:128], MP[:, :, :, :, :].rearrange("p a b c g -> p (a b c g)"),
                                    IDH[:, :]).then_inc(mtr_done, 1)

            def step(t, par, tt):
                nxt = 1 - par
                for c in range(NC):
                    if has(tt, 1):
                        if c == 0:
                            pe.wait_ge(kts_ld[nxt], 16 * turn(t, par, 1))
                            pe.wait_ge(qt_ready, 2 * (t + 1) + 1)
                        if c == 4:
                            pe.wait_ge(qt_ready, 2 * (t + 1) + 2)
                        if tt != -1 or c >= 2:
                            pe.wait_ge(max_done, NC * (t + 1) + c - 1)
                        scores(t + 1, c, nxt)
                    if has(tt, 0):
                        if c == 0:
                            pe.wait_ge(ktt_ld[par], 16 * turn(t, par, 0))
                            pe.wait_ge(m_ld[0], 16 * (t + 1))
                        if c == 4:
                            pe.wait_ge(m_ld[1], 16 * (t + 1))
                        if tt != 0 or c >= 2:
                            pe.wait_ge(exp_done, NC * t + c - 1)
                        shifted(t, c, par)
                    if c == 0:
                        if has(tt, 0):
                            if tt is None or tt >= 0:
                                pe.wait_ge(mt_ready, 2 * t + 1)
                            shift_back(t, 1)
                        if has(tt, 1):
                            pe.wait_ge(qt_ready, 2 * (t + 1) + 1)
                            stack(t + 1, 1)
                    if c == 1 and has(tt, -1):
                        pe.wait_ge(exp_done, NC * t)
                        pe.wait_ge(os_ready, 2 * t - 1)
                        sums(t - 1, 1, nxt)
                    if c == 3 and has(tt, -1):
                        pe.wait_ge(ao_ready, 2 * t - 1)
                        queries_back(t - 1, 1)
                    if c == 4 and has(tt, 1):
                        if tt != -1:
                            pe.wait_ge(mt_ready, 2 * (t + 1))
                        shift_back(t + 1, 0)
                    if c == 4 and has(tt, 0):
                        pe.wait_ge(v_ld[par], 16 * turn(t, par, 0))
                        pe.wait_ge(exp_done, NC * t + 4)
                        if tt != 0:
                            pe.wait_ge(os_ready, 2 * t)
                        sums(t, 0, par)
                    if c == 5 and has(tt, 2):
                        if tt != -2:
                            pe.wait_ge(qt_ready, 2 * (t + 2))
                        stack(t + 2, 0)
                    if c == 6 and has(tt, 0):
                        if tt != 0:
                            pe.wait_ge(ao_ready, 2 * t)
                        queries_back(t, 0)
            steps(pe, step)

            pe.wait_ge(sign_done, 2)
            for i in range(4):
                if i:
                    pe.wait_ge(wt_ready, i)
                for a in range(8):
                    if i < FC:
                        src = SU[:, a, i * 128:(i + 1) * 128]
                    else:
                        k, c = 4 * (i - FC) + a // FC, a % FC
                        src = SD[:, c, k * 128:(k + 1) * 128]
                    last = nc.tensor.transpose(PQh[:, a * 128:(a + 1) * 128], src, IDH[:, :])
                last.then_inc(wtr_done, 1)

            def tokens(n):
                for p in range(2):
                    if p == 0:
                        pe.wait_ge(xh_ready, n + 1)
                        if n:
                            pe.wait_ge(xt_ready, 2 * n)
                        else:
                            pe.wait_ge(wt_ready, 4)
                    else:
                        pe.wait_ge(xl_ready, n + 1)
                        pe.wait_ge(xt_ready, 2 * n + 1)
                    for c in range(FC):
                        for i in range(GB):
                            a = c * GB + i
                            last = nc.tensor.transpose(PQh[:, a * 128:(a + 1) * 128],
                                                       XH[:, p, i, c * 128:(c + 1) * 128], IDH[:, :])
                    last.then_inc(xtr_done, 1)

            def up(n, k):
                m = n * HK + k
                if k == 0:
                    pe.wait_ge(xt_ready, 2 * n + 2)
                if m == 0:
                    pe.wait_ge(max_done, NC * B)
                    pe.wait_ge(mt_ready, 2 * B)
                if m >= 3:
                    pe.wait_ge(hh_ready, m - 2)
                for p in range(2):
                    for c in range(FC):
                        last = nc.tensor.matmul(UPB[m % 3][:, :], UT[:, c, k * 128:(k + 1) * 128], XT[:, p, c, :],
                                                start=(p == 0 and c == 0), stop=(p == 1 and c == FC - 1))
                last.then_inc(up_done, 1)

            def down(n, k):
                m = n * HK + k
                pe.wait_ge(hl_ready, m + 1)
                for i in range(GB):
                    if k == 0:
                        if n:
                            pe.wait_ge(ys_ready, (n - 1) * GB + i + 1)
                        elif i == 0:
                            pe.wait_ge(exp_done, NC * B)
                            pe.wait_ge(os_ready, 2 * B)
                            pe.wait_ge(ao_ready, 2 * B)
                    for p in range(2):
                        last = nc.tensor.matmul(YB[i][:, 0:E], HP[m % 4][:, p, i * 128:(i + 1) * 128], DT[:, k, :],
                                                start=(k == 0 and p == 0), stop=(k == HK - 1 and p == 1))
                    if k == HK - 1:
                        last.then_inc(y_done, 1)
                if k < HK - 1:
                    last.then_inc(down_k, 1)

            tokens(0)
            for n in range(NG):
                for k in range(HK):
                    up(n, k)
                    if k >= 2:
                        down(n, k - 2)
                if n + 1 < NG:
                    tokens(n + 1)
                down(n, HK - 2)
                down(n, HK - 1)


_INS = ['x', 'ctx_512', 'g_xattn', 'g_ffn', 'L0_ffn_up_weight', 'L0_ffn_down_weight', 'L0_ffn_up_scale',
        'L0_ffn_down_scale', 'L0_ffn_output_scale']


def kernel(**inputs):
    import numpy as _np
    import concourse.bacc as _bacc
    from concourse import mybir as _mybir
    from concourse.bass_utils import run_bass_kernel_spmd as _run

    nc = _bacc.Bacc("TRN2", target_bir_lowering=False, num_devices=1)
    arrays, args = {}, []
    for name in _INS:
        a = _np.ascontiguousarray(inputs[name])
        arrays[f"in_{name}"] = a
        args.append(nc.dram_tensor(f"in_{name}", a.shape, _mybir.dt.from_np(a.dtype), kind="ExternalInput").ap())
    args.append(nc.dram_tensor("out_0", inputs['x'].shape, _mybir.dt.float32, kind="ExternalOutput").ap())
    flamingo_kernel(nc, *args)
    r = _run(nc, [arrays], core_ids=[0])
    return r.results[0]["out_0"]
```

```python
import concourse.bass as bass
from concourse import mybir
from contextlib import ExitStack


def flamingo_kernel(nc: bass.Bass, x, ctx_in, g_xattn, g_ffn, up_w, down_w, up_s, down_s, out_s, out):
    fp32, bf16, fp16 = mybir.dt.float32, mybir.dt.bfloat16, mybir.dt.float16
    ALU, ACT, AX = mybir.AluOpType, mybir.ActivationFunctionType, mybir.AxisListType

    B, S, E = x.shape
    KF = ctx_in.shape[2]
    D = 8
    KVH = KF // D
    QH = E // D
    G = QH // KVH
    JP = KVH // 2
    HID = up_w.shape[0]
    HK = HID // 128
    FC = E // 128
    GB = 4
    NG = B // GB
    EPS = 1e-5
    SCALE = float(D) ** -0.5
    SHIFT = float(2 ** 20)
    UP_TARGET = 64.0
    ONE = 3 * D
    NC = KVH
    PIPE = 2

    es = ExitStack()
    with es:
        def sb(name, shape, dt):
            return es.enter_context(nc.sbuf_tensor(name, shape, dt))

        def pb(name, shape, dt):
            return es.enter_context(nc.psum_tensor(name, shape, dt))

        def sem(name):
            return es.enter_context(nc.semaphore(name))

        X = sb("X", [128, B, E], fp32)
        CTX = sb("CTX", [128, B, KF], fp32)
        KP = sb("KP", [128, B * KVH, 2, 32], bf16)
        KR = sb("KR", [128, B * KVH, D], fp32)
        KTA = sb("KTA", [128, B, JP * 128], bf16)
        KTS = [sb(f"KTS{i}", [128, JP, 128], bf16) for i in range(2)]
        KTT = [sb(f"KTT{i}", [128, JP, 128], bf16) for i in range(2)]
        VA = sb("VA", [128, B, KVH * 32], fp32)
        V = [sb(f"V{i}", [128, KVH, 32], fp32) for i in range(2)]
        Q = sb("Q", [128, QH, D], fp32)
        QS = sb("QS", [128, QH, 2, 32], fp16)
        QT = [sb(f"QT{i}", [128, JP, G * 128], fp16) for i in range(2)]
        NM = [sb(f"NM{i}", [128, 2, 2, 2, G], fp32) for i in range(2)]
        MP = sb("MP", [128, 2, 2, 2, G], fp16)
        MT = [sb(f"MT{i}", [32, 128], fp16) for i in range(2)]
        P = [sb(f"P{i}", [128, KVH, G * 128], fp32) for i in range(2)]
        OS = [sb(f"OS{i}", [128, G * 128], fp32) for i in range(2)]
        RC = [sb(f"RC{i}", [128, G, 4], fp32) for i in range(2)]
        AO = [sb(f"AO{i}", [128, 2, 4, G, D], fp32) for i in range(2)]
        ST1 = sb("ST1", [128, B, 6], fp32)
        MV1 = sb("MV1", [128, B, 2], fp32)
        VE1 = sb("VE1", [128, B], fp32)
        RS1 = sb("RS1", [128, B], fp32)
        MR1 = sb("MR1", [128, B], fp32)
        NB1 = sb("NB1", [128, B], fp32)
        HALF = sb("HALF", [128, B], fp32)
        IDF = sb("IDF", [128, 128], fp32)
        IDH = sb("IDH", [128, 128], fp16)
        IDB = sb("IDB", [128, 128], bf16)
        GX = sb("GX", [128, 1], fp32)
        TX = sb("TX", [128, 1], fp32)
        GF = sb("GF", [128, 1], fp32)
        TF = sb("TF", [128, 1], fp32)
        OSC = sb("OSC", [128, 1], fp32)
        DS = sb("DS", [128, E], fp32)
        CS = sb("CS", [128, E], fp32)
        US = sb("US", [128, HK], fp32)
        UN = sb("UN", [128, HK], fp32)
        um = sb("um", [128, 1], fp32)
        uma = sb("uma", [128, 1], fp32)
        umg = sb("umg", [128, 1], fp32)
        umr = sb("umr", [128, 1], fp32)
        fac = sb("fac", [128, 1], fp32)
        UW = sb("UW", [128, HK, E], fp32)
        DW = sb("DW", [128, FC, HID], fp32)
        NEG = [sb(f"NEG{i}", [128, HK * E], fp16) for i in range(2)]
        SU = sb("SU", [128, HK, E], fp16)
        SD = sb("SD", [128, FC, HID], fp16)
        UT = sb("UT", [128, FC, HID], fp16)
        DT = sb("DT", [128, HK, E], fp16)
        WF = [w[:, :, :].rearrange("p a b -> p (a b)") for w in (UW, DW)]
        WS = [w[:, :, :].rearrange("p a b -> p (a b)") for w in (SU, SD)]
        ST2 = sb("ST2", [128, GB, 6], fp32)
        MV2 = sb("MV2", [128, GB, 2], fp32)
        VE2 = sb("VE2", [128, GB], fp32)
        RS2 = sb("RS2", [128, GB], fp32)
        XN = sb("XN", [128, GB, E], fp32)
        XH = sb("XH", [128, 2, GB, E], fp16)
        XT = sb("XT", [128, 2, FC, GB * 128], fp16)
        HF = [sb(f"HF{i}", [128, 512], fp32) for i in range(2)]
        HP = [sb(f"HP{i}", [128, 2, 512], fp16) for i in range(4)]
        YS = sb("YS", [128, GB, E], fp32)

        PS_ = [pb(f"PS{i}", [128, 512], fp32) for i in range(2)]
        PT_ = [pb(f"PT{i}", [128, 512], fp32) for i in range(2)]
        PQ = pb("PQ", [128, 512], fp32)
        PM = pb("PM", [128, 512], fp32)
        PO = pb("PO", [128, 512], fp32)
        PX = pb("PX", [128, 512], fp32)
        PQh, PQb, PMh = PQ[:, :].bitcast(fp16), PQ[:, :].bitcast(bf16), PM[:, :].bitcast(fp16)
        KBANK = [b[:, :].bitcast(bf16) for b in (PQ, PM, PO, PX)]
        SBANK = [b[:, :].bitcast(fp16) for b in (PS_[0], PS_[1], PQ, PS_[0])]
        UPB = [PS_[0], PS_[1], PM]
        YB = [PT_[0], PT_[1], PO, PX]

        ld_ctx = sem("ld_ctx")
        ld_x = [sem(f"ld_x{i}") for i in range(NG)]
        ld_small = sem("ld_small")
        ld_g = sem("ld_g")
        ld_w = [sem(f"ld_w{i}") for i in range(2)]
        ident = sem("ident")
        zeroed = sem("zeroed")
        k_hi, k_r1, k_mid, k_r2, k_lo = (sem(n) for n in ("k_hi", "k_r1", "k_mid", "k_r2", "k_lo"))
        v_ready = sem("v_ready")
        k_tr, k_ev = sem("k_tr"), [sem(f"k_ev{i}") for i in range(2)]
        st_ready, mv_ready, ve_ready, rs_ready, mr_ready, nb_ready = (
            sem(n) for n in ("st_ready", "mv_ready", "ve_ready", "rs_ready", "mr_ready", "nb_ready"))
        tx_ready = sem("tx_ready")
        q_ready, hi_ready, lo_ready = sem("q_ready"), sem("hi_ready"), sem("lo_ready")
        qtr_done, qt_ready = sem("qtr_done"), [sem(f"qt_ready{i}") for i in range(2)]
        kts_ld = [sem(f"kts_ld{i}") for i in range(2)]
        ktt_ld = [sem(f"ktt_ld{i}") for i in range(2)]
        v_ld = [sem(f"v_ld{i}") for i in range(2)]
        s_done, max_done = sem("s_done"), sem("max_done")
        mh_ready, mp_ready, mtr_done, mt_ready = sem("mh_ready"), sem("mp_ready"), sem("mtr_done"), sem("mt_ready")
        m_ld = [sem(f"m_ld{i}") for i in range(2)]
        t_done, exp_done = sem("t_done"), sem("exp_done")
        pv_done, os_ready, otr_done = sem("pv_done"), sem("os_ready"), sem("otr_done")
        rc_ready, ao_ready, x1_ready = sem("rc_ready"), sem("ao_ready"), sem("x1_ready")
        neg_done, sign_done = sem("neg_done"), sem("sign_done")
        wtr_done, wt_ready = sem("wtr_done"), sem("wt_ready")
        um_ready, uma_ready, us_step, un_ready, cs_ready = (
            sem(n) for n in ("um_ready", "uma_ready", "us_step", "un_ready", "cs_ready"))
        st2_ready, mv2_ready, ve2_ready, rs2_ready, xn_ready, xh_ready, xl_ready = (
            sem(n) for n in ("st2_ready", "mv2_ready", "ve2_ready", "rs2_ready", "xn_ready", "xh_ready", "xl_ready"))
        xtr_done, xt_ready = sem("xtr_done"), sem("xt_ready")
        up_done, h_ready, hh_ready, hl_ready, down_done, y_done = (
            sem(n) for n in ("up_done", "h_ready", "hh_ready", "hl_ready", "down_done", "y_done"))
        ys_ready, y_ready, stored = sem("ys_ready"), sem("y_ready"), sem("stored")

        block = es.enter_context(nc.Block())

        HEAD, TAIL = (-2, -1, 0, 1), (B - 2, B - 1, B)
        LOOP = (2, B - 2)

        def steps(engine, step):
            for t in HEAD:
                step(t, t % 2, t)
            with engine.Fori(0, (LOOP[1] - LOOP[0]) // PIPE) as i:
                for u in range(PIPE):
                    step(i * PIPE + LOOP[0] + u, (LOOP[0] + u) % 2, None)
            for t in TAIL:
                step(t, t % 2, t)

        def has(t, d):
            return t is None or 0 <= t + d < B

        def turn(t, par, d):
            odd = (par + d) % 2
            return (t + d - odd) // 2 + 1 if isinstance(t, int) else (t + (d - odd)) // 2 + 1

        @block.sync
        def _(sp):
            sp.dma_start(CTX[:, :, :], ctx_in.rearrange("b s f -> s b f")).then_inc(ld_ctx, 16)
            for n in range(NG):
                sp.dma_start(X[:, n * GB:(n + 1) * GB, :],
                             x[n * GB:(n + 1) * GB, :, :].rearrange("b s f -> s b f")).then_inc(ld_x[n], 16)
            sp.dma_start(UW[:, :, :], up_w.rearrange("(k p) f -> p k f", p=128)).then_inc(ld_w[0], 16)
            sp.dma_start(DW[:, :, :], down_w.rearrange("(c p) h -> p c h", p=128)).then_inc(ld_w[1], 16)

            def shift_rows(b, hf, par):
                sp.dma_start(QT[par][ONE:128:32, 2 * hf:2 * hf + 2, :], MT[hf][:, :]).then_inc(m_ld[hf], 16)

            def step(t, par, tt):
                nxt = 1 - par
                if has(tt, 2):
                    if tt is None or tt >= 0:
                        sp.wait_ge(s_done, NC * (t + 1))
                    if tt == -2:
                        sp.wait_ge(k_ev[0], B // 4)
                        sp.wait_ge(k_ev[1], B // 4)
                    sp.dma_start(KTS[par][:, :, :], KTA[:, bass.ds(t + 2, 1), :].rearrange(
                        "p o (j t) -> p (o j) t", j=JP)).then_inc(kts_ld[par], 16)
                if has(tt, 1):
                    if tt is None or tt >= 1:
                        sp.wait_ge(t_done, NC * t)
                    sp.dma_start(KTT[nxt][:, :, :], KTA[:, bass.ds(t + 1, 1), :].rearrange(
                        "p o (j t) -> p (o j) t", j=JP)).then_inc(ktt_ld[nxt], 16)
                if has(tt, 0):
                    sp.wait_ge(mt_ready, 2 * t + 2)
                    shift_rows(t, 1, par)
                if has(tt, 1):
                    if tt == -1:
                        sp.wait_ge(v_ready, 3)
                    if tt is None or tt >= 1:
                        sp.wait_ge(pv_done, 2 * t)
                    sp.dma_start(V[nxt][:, :, :], VA[:, bass.ds(t + 1, 1), :].rearrange(
                        "p o (j c) -> p (o j) c", j=KVH)).then_inc(v_ld[nxt], 16)
                    sp.wait_ge(mt_ready, 2 * (t + 1) + 1)
                    shift_rows(t + 1, 0, nxt)
            steps(sp, step)

            for n in range(NG):
                for i in range(GB):
                    sp.wait_ge(y_ready, n * GB + i + 1)
                    sp.dma_start(out[n * GB + i, :, :], X[:, n * GB + i, :]).then_inc(stored, 16)
            sp.wait_ge(stored, 16 * B)

        @block.gpsimd
        def _(pool):
            nc.gpsimd.memset(IDF[:, :], 0.0).then_inc(zeroed, 1)
            pool.wait_ge(zeroed, 1)
            nc.gpsimd.affine_select(out=IDF[:, :], in_=IDF[:, :], compare_op=ALU.not_equal, fill=1.0, base=0,
                                    pattern=[[-1, 128]], channel_multiplier=1).then_inc(ident, 1)
            nc.gpsimd.memset(HALF[:, :], -0.5).then_inc(x1_ready, 1)
            va = VA[:, :, :].rearrange("p b (j c) -> p (b j) c", c=32)
            nc.gpsimd.memset(va[:, :, D:D + 1], 1.0).then_inc(v_ready, 1)
            nc.gpsimd.memset(va[:, :, D + 1:32], 0.0).then_inc(v_ready, 1)

            def inverse_roots(n):
                r = slice(n * GB, (n + 1) * GB)
                pool.wait_ge(x1_ready, 1)
                pool.wait_ge(ve_ready, n + 1)
                nc.gpsimd.tensor_tensor(RS1[:, r], VE1[:, r], HALF[:, r], ALU.pow).then_inc(rs_ready, 1)

            def negative(n):
                pool.wait_ge(ld_w[n], 16)
                nc.gpsimd.tensor_scalar(NEG[n][:, :], WF[n], 0.0, None, ALU.is_lt).then_inc(neg_done, 1)

            def step(t, par, tt):
                if tt == -2:
                    inverse_roots(0)
                if has(tt, 2):
                    pool.wait_ge(hi_ready, t + 3)
                    nc.gpsimd.tensor_tensor(
                        QS[:, :, 1, 0:ONE].rearrange("p h (r d) -> p h r d", d=D),
                        Q[:, :, :].rearrange("p h (o d) -> p h o d", o=1).to_broadcast([128, QH, 3, D]),
                        QS[:, :, 0, 0:ONE].rearrange("p h (r d) -> p h r d", d=D),
                        ALU.subtract).then_inc(lo_ready, 1)
                if tt in (-2, -1, 0):
                    inverse_roots(tt + 3)
                if tt == B - 1:
                    pool.wait_ge(ve2_ready, 1)
                    nc.gpsimd.tensor_tensor(RS2[:, :], VE2[:, :], HALF[:, 0:GB], ALU.pow).then_inc(rs2_ready, 1)
                if has(tt, -1):
                    pool.wait_ge(ao_ready, 2 * t)
                    xb = X[:, bass.ds(t - 1, 1), :].rearrange("p o f -> p (o f)")
                    nc.gpsimd.tensor_tensor(xb, xb, AO[1 - par][:, :, :, :, :].rearrange("p h c g d -> p (h c g d)"),
                                            ALU.add).then_inc(x1_ready, 1)
                if tt == -2:
                    pool.wait_ge(um_ready, 1)
                    nc.gpsimd.partition_all_reduce(uma[:, :], um[:, :], 128,
                                                   bass.bass_isa.ReduceOp.max).then_inc(uma_ready, 1)
                if tt in (0, 1):
                    negative(tt)
            steps(pool, step)

            with pool.Fori(0, NG - 1) as n:
                pool.wait_ge(ve2_ready, n + 2)
                nc.gpsimd.tensor_tensor(RS2[:, :], VE2[:, :], HALF[:, 0:GB], ALU.pow).then_inc(rs2_ready, 1)

        @block.scalar
        def _(act):
            act.dma_start(GX[:, :], g_xattn[None, :].to_broadcast([128, 1])).then_inc(ld_g, 16)
            act.dma_start(GF[:, :], g_ffn[None, :].to_broadcast([128, 1])).then_inc(ld_g, 16)
            act.dma_start(OSC[:, :], out_s[None, :].to_broadcast([128, 1])).then_inc(ld_small, 16)
            act.dma_start(DS[:, :], down_s[None, :].to_broadcast([128, E])).then_inc(ld_small, 16)
            act.dma_start(US[:, :], up_s.rearrange("(k p) -> p k", p=128),
                          allow_slow_non_contiguous=True).then_inc(ld_small, 16)
            act.wait_ge(k_r1, 1)
            nc.scalar.copy(KP[:, :, 0, D:2 * D], KR[:, :, :]).then_inc(k_mid, 1)
            act.wait_ge(ld_g, 32)
            nc.scalar.activation(TX[:, :], GX[:, :], ACT.Tanh).then_inc(tx_ready, 1)
            nc.scalar.activation(TF[:, :], GF[:, :], ACT.Tanh).then_inc(tx_ready, 1)
            act.wait_ge(tx_ready, 1)
            nc.scalar.mul(VA[:, :, :].rearrange("p b (j c) -> p (b j) c", c=32)[:, :, 0:D],
                          CTX[:, :, :].rearrange("p b (j d) -> p (b j) d", d=D), TX[:, 0:1]).then_inc(v_ready, 1)
            for i in range(1, B // 2, 2):
                act.wait_ge(k_tr, i + 1)
                nc.scalar.copy(KTA[:, 2 * i:2 * i + 2, :].rearrange("p b n -> p (b n)"),
                               KBANK[i % 4][:, 0:1024]).then_inc(k_ev[1], 1)

            def layer_norm(b):
                for side in range(2):
                    nc.scalar.activation(
                        Q[:, :, :].rearrange("p (j g s) d -> p j g s d", j=JP, s=2)[:, :, :, side, :],
                        X[:, bass.ds(b, 1), :].rearrange(
                            "p o (j s g d) -> p (o j) s g d", j=JP, s=2, d=D)[:, :, side, :, :],
                        ACT.Identity, bias=NB1[:, bass.ds(b, 1)],
                        scale=RS1[:, bass.ds(b, 1)]).then_inc(q_ready, 1)

            def step(t, par, tt):
                if has(tt, 2):
                    if tt in HEAD:
                        act.wait_ge(nb_ready, 1)
                    if tt is None or tt >= -1:
                        act.wait_ge(lo_ready, t + 2)
                    layer_norm(t + 2)
                for c in range(NC):
                    if has(tt, 0):
                        act.wait_ge(t_done, NC * t + c + 1)
                        if tt is None or tt >= 2:
                            if c % 4 == 0:
                                act.wait_ge(pv_done, 2 * (t - 2) + c // 4 + 1)
                        nc.scalar.activation(P[par][:, c, :], PT_[c % 2][:, :], ACT.Exp,
                                             scale=SCALE).then_inc(exp_done, 1)
                    if c == 0 and has(tt, 2):
                        act.wait_ge(q_ready, 2 * (t + 3))
                        if tt != -2:
                            act.wait_ge(qtr_done, 2 * (t + 2))
                        nc.scalar.copy(QS[:, :, 0, 0:ONE].rearrange("p h (r d) -> p h r d", d=D),
                                       Q[:, :, :].rearrange("p h (o d) -> p h o d", o=1).to_broadcast(
                                           [128, QH, 3, D])).then_inc(hi_ready, 1)
                    if c == 2 and has(tt, -1):
                        act.wait_ge(pv_done, 2 * t)
                        if tt != 1:
                            act.wait_ge(otr_done, 2 * t - 2)
                        nc.scalar.copy(OS[1][:, :], PO[:, :]).then_inc(os_ready, 1)
                    if c == 5 and has(tt, 2):
                        act.wait_ge(qtr_done, 2 * (t + 2) + 1)
                        if tt is None or tt >= 0:
                            act.wait_ge(t_done, NC * t + 4)
                        nc.scalar.copy(QT[par][:, 0:2, :].rearrange("p a n -> p (a n)"),
                                       PQh[:, 0:1024]).then_inc(qt_ready[0], 1)
                    if c == 6 and has(tt, 0):
                        act.wait_ge(pv_done, 2 * t + 1)
                        if tt is None or tt >= 1:
                            act.wait_ge(otr_done, 2 * t - 1)
                        nc.scalar.copy(OS[0][:, :], PO[:, :]).then_inc(os_ready, 1)
                if tt == HEAD[-1]:
                    act.wait_ge(nb_ready, NG)
                if tt == B - 1:
                    act.wait_ge(xn_ready, 1)
                    nc.scalar.copy(XH[:, 0, :, :], XN[:, :, :]).then_inc(xh_ready, 1)
            steps(act, step)

            def hidden(n, k, first, more):
                act.wait_ge(up_done, n * HK + k + 1)
                if k >= 2 or not first:
                    act.wait_ge(hl_ready, n * HK + k - 1)
                nc.scalar.activation(HF[k % 2][:, :], UPB[k % 3][:, :], ACT.Relu,
                                     scale=UN[:, k:k + 1]).then_inc(h_ready, 1)
                if k >= 4:
                    act.wait_ge(down_done, n * (HK - 1) + k - 3)
                elif k == 3 and not first:
                    act.wait_ge(y_done, n * GB)
                elif not first:
                    act.wait_ge(down_done, n * (HK - 1) + k - 2)
                nc.scalar.activation(HP[k % 4][:, 0, :], UPB[k % 3][:, :], ACT.Relu,
                                     scale=UN[:, k:k + 1]).then_inc(hh_ready, 1)
                if k == 4 and more:
                    act.wait_ge(xn_ready, n + 2)
                    act.wait_ge(xtr_done, 2 * n + 2)
                    nc.scalar.copy(XH[:, 0, :, :], XN[:, :, :]).then_inc(xh_ready, 1)

            act.wait_ge(un_ready, 1)
            for k in range(HK):
                hidden(0, k, True, True)
            with act.Fori(1, NG - 1) as n:
                for k in range(HK):
                    hidden(n, k, False, True)
            for k in range(HK):
                hidden(NG - 1, k, False, False)

        @block.vector
        def _(dve):
            CX = CTX[:, :, :].rearrange("p b (j d) -> p (b j) d", d=D)
            nc.vector.memset(KP[:, :, 0, ONE + 1:32], 0.0)
            nc.vector.memset(KP[:, :, 0, ONE:ONE + 1], SHIFT)
            nc.vector.memset(QS[:, :, :, ONE:32], 0.0)
            dve.wait_ge(ident, 1)
            nc.vector.tensor_copy(IDH[:, :], IDF[:, :])
            nc.vector.tensor_copy(IDB[:, :], IDF[:, :]).then_inc(ident, 1)
            dve.wait_ge(ld_ctx, 16)
            nc.vector.tensor_copy(KP[:, :, 0, 0:D], CX).then_inc(k_hi, 1)
            dve.wait_ge(k_hi, 1)
            nc.vector.tensor_tensor(KR[:, :, :], CX, KP[:, :, 0, 0:D], ALU.subtract).then_inc(k_r1, 1)
            dve.wait_ge(k_mid, 1)
            nc.vector.tensor_tensor(KP[:, :, 0, 2 * D:3 * D], KR[:, :, :], KP[:, :, 0, D:2 * D],
                                    ALU.subtract).then_inc(k_lo, 1)
            dve.wait_ge(k_lo, 1)
            nc.vector.tensor_copy(KP[:, :, 1, :], KP[:, :, 0, :]).then_inc(k_lo, 1)

            def statistics(n):
                r = slice(n * GB, (n + 1) * GB)
                dve.wait_ge(ld_x[n], 16)
                for b in range(n * GB, (n + 1) * GB):
                    nc.vector.bn_stats(ST1[:, b, :], X[:, b, :]).then_inc(st_ready, 1)
                for b in range(n * GB, (n + 1) * GB):
                    dve.wait_ge(st_ready, b + 1)
                    nc.vector.bn_aggr(MV1[:, b, :], ST1[:, b, :]).then_inc(mv_ready, 1)
                dve.wait_ge(mv_ready, (n + 1) * GB)
                nc.vector.tensor_scalar(VE1[:, r], MV1[:, r, 1], EPS, None, ALU.add).then_inc(ve_ready, 1)

            def offsets(n):
                r = slice(n * GB, (n + 1) * GB)
                dve.wait_ge(rs_ready, n + 1)
                nc.vector.scalar_tensor_tensor(NB1[:, r], MV1[:, r, 0], -1.0, RS1[:, r], ALU.mult,
                                               ALU.mult).then_inc(nb_ready, 1)

            statistics(0)
            for i in range(0, B // 2, 2):
                dve.wait_ge(k_tr, i + 1)
                nc.vector.tensor_copy(KTA[:, 2 * i:2 * i + 2, :].rearrange("p b n -> p (b n)"),
                                      KBANK[i % 4][:, 0:1024]).then_inc(k_ev[0], 1)
                if i == 0:
                    offsets(0)

            def largest_scale():
                dve.wait_ge(ld_small, 48)
                nc.vector.tensor_reduce(um[:, :], US[:, :], AX.X, ALU.max,
                                        apply_absolute_value=True).then_inc(um_ready, 1)

            def output_factors():
                dve.wait_ge(uma_ready, 1)
                nc.vector.tensor_scalar(umg[:, :], uma[:, :], 1e-30, None, ALU.max).then_inc(us_step, 1)
                dve.wait_ge(us_step, 1)
                nc.vector.reciprocal(umr[:, :], umg[:, :]).then_inc(us_step, 1)
                dve.wait_ge(us_step, 2)
                nc.vector.tensor_scalar(UN[:, :], US[:, :], umr[:, 0:1], UP_TARGET, ALU.mult,
                                        ALU.mult).then_inc(un_ready, 1)
                dve.wait_ge(tx_ready, 2)
                nc.vector.tensor_scalar(fac[:, :], umg[:, :], TF[:, 0:1], 1.0 / UP_TARGET, ALU.mult,
                                        ALU.mult).then_inc(us_step, 1)
                dve.wait_ge(us_step, 3)
                nc.vector.tensor_scalar(CS[:, :], DS[:, :], OSC[:, 0:1], fac[:, 0:1], ALU.mult,
                                        ALU.mult).then_inc(cs_ready, 1)

            def sign(n):
                dve.wait_ge(neg_done, n + 1)
                nc.vector.scalar_tensor_tensor(WS[n], WF[n], 0.0, NEG[n][:, :], ALU.is_gt,
                                               ALU.subtract).then_inc(sign_done, 1)

            def signs_out(i):
                dve.wait_ge(wtr_done, i + 1)
                dst = UT[:, i, :] if i < FC else DT[:, 4 * (i - FC):4 * (i - FC) + 4, :].rearrange("p k n -> p (k n)")
                nc.vector.tensor_copy(dst, SBANK[i][:, 0:1024]).then_inc(wt_ready, 1)

            def tokens_at(n, i):
                return X[:, bass.ds(n * GB + i, 1), :].rearrange("p o f -> p (o f)")

            def norm_group(n):
                dve.wait_ge(x1_ready, n * GB + GB + 1)
                for i in range(GB):
                    nc.vector.bn_stats(ST2[:, i, :], tokens_at(n, i)).then_inc(st2_ready, 1)

            def aggregate_group(n):
                for i in range(GB):
                    nc.vector.bn_aggr(MV2[:, i, :], ST2[:, i, :]).then_inc(mv2_ready, 1)
                dve.wait_ge(mv2_ready, n * GB + GB)
                nc.vector.tensor_scalar(VE2[:, :], MV2[:, :, 1], EPS, None, ALU.add).then_inc(ve2_ready, 1)

            def apply_group(n):
                dve.wait_ge(rs2_ready, n + 1)
                for i in range(GB):
                    last = nc.vector.tensor_scalar(XN[:, i, :], tokens_at(n, i), MV2[:, i, 0:1], RS2[:, i:i + 1],
                                                   ALU.subtract, ALU.mult)
                last.then_inc(xn_ready, 1)

            def low_group(n):
                dve.wait_ge(xh_ready, n + 1)
                nc.vector.tensor_tensor(XH[:, 1, :, :], XN[:, :, :], XH[:, 0, :, :], ALU.subtract).then_inc(xl_ready, 1)

            def tokens_out(n, p, first):
                dve.wait_ge(xtr_done, 2 * n + p + 1)
                if p == 0 and not first:
                    dve.wait_ge(up_done, HK * n)
                nc.vector.tensor_copy(XT[:, p, :, :].rearrange("p c n -> p (c n)"), PQh[:, 0:1024]).then_inc(xt_ready, 1)

            def maxima(t, c, par):
                dve.wait_ge(s_done, NC * t + c + 1)
                nc.vector.tensor_reduce(NM[par][:, c // 4, c % 2, c // 2 % 2, :], PS_[c % 2][:, :].rearrange(
                    "p (g t) -> p g t", g=G), AX.X, ALU.max, negate=True).then_inc(max_done, 1)

            def shift_high(b, hf, par, first):
                dve.wait_ge(max_done, NC * b + 4 * hf + 4)
                if not first:
                    dve.wait_ge(mtr_done, 2 * b + hf)
                nc.vector.tensor_scalar(MP[:, :, 0, :, :].rearrange("p s a g -> p s (a g)"),
                                        NM[par][:, hf, :, :, :].rearrange("p s a g -> p s (a g)"), 1.0 / SHIFT, None,
                                        ALU.mult).then_inc(mh_ready, 1)

            def shift_low(b, hf, par):
                dve.wait_ge(mh_ready, 2 * b + hf + 1)
                nc.vector.scalar_tensor_tensor(MP[:, :, 1, :, :].rearrange("p s a g -> p s (a g)"),
                                               NM[par][:, hf, :, :, :].rearrange("p s a g -> p s (a g)"), 1.0 / SHIFT,
                                               MP[:, :, 0, :, :].rearrange("p s a g -> p s (a g)"), ALU.mult,
                                               ALU.subtract).then_inc(mp_ready, 1)

            def shift_out(b, hf, first):
                dve.wait_ge(mtr_done, 2 * b + hf + 1)
                if not first:
                    dve.wait_ge(m_ld[hf], 16 * b)
                nc.vector.tensor_copy(MT[hf][:, :], PMh[0:32, 0:128]).then_inc(mt_ready, 1)

            def stacked_out(b, r, par, old):
                dve.wait_ge(qtr_done, 2 * b + r + 1)
                if old:
                    dve.wait_ge(t_done, NC * (b - 2) + 4 * r + 4)
                nc.vector.tensor_copy(QT[par][:, 2 * r:2 * r + 2, :].rearrange("p a n -> p (a n)"),
                                      PQh[:, 0:1024]).then_inc(qt_ready[r], 1)

            by_head = PX[:, :].rearrange("p (g c r) -> p g c r", g=G, c=4)

            def reciprocals(b, hf):
                dve.wait_ge(otr_done, 2 * b + hf + 1)
                nc.vector.reciprocal(RC[hf][:, :, :], by_head[:, :, :, D]).then_inc(rc_ready, 1)

            def normalise(b, hf, par, old):
                dve.wait_ge(rc_ready, 2 * b + hf + 1)
                if old:
                    dve.wait_ge(x1_ready, b)
                nc.vector.tensor_tensor(
                    AO[par][:, hf, :, :, :].rearrange("p c g d -> p g c d"), by_head[:, :, :, 0:D],
                    RC[hf][:, :, :].rearrange("p g (c o) -> p g c o", o=1).to_broadcast([128, G, 4, D]),
                    ALU.mult).then_inc(ao_ready, 1)

            def step(t, par, tt):
                nxt = 1 - par
                for c in range(NC):
                    if c == 2 and has(tt, 1):
                        stacked_out(t + 1, 1, nxt, tt is None or tt >= 1)
                    if has(tt, 1):
                        maxima(t + 1, c, nxt)
                    if c == 0 and has(tt, 0):
                        shift_out(t, 1, tt == 0)
                    if c == 3 and has(tt, 1):
                        shift_high(t + 1, 0, nxt, tt == -1)
                    if c == 3 and has(tt, -1):
                        reciprocals(t - 1, 0)
                    if c == 3 and has(tt, 1):
                        shift_low(t + 1, 0, nxt)
                    if c == 4 and has(tt, -1):
                        normalise(t - 1, 0, nxt, tt is None or tt >= 3)
                    if c == 5 and has(tt, 1):
                        shift_out(t + 1, 0, tt == -1)
                    if c == 7 and has(tt, -1):
                        reciprocals(t - 1, 1)
                    if c == 7 and has(tt, 1):
                        shift_high(t + 1, 1, nxt, False)
                    if c == 7 and has(tt, -1):
                        normalise(t - 1, 1, nxt, False)
                    if c == 7 and has(tt, 1):
                        shift_low(t + 1, 1, nxt)
                    if tt == B - 1:
                        if c == 0:
                            norm_group(0)
                            sign(0)
                            dve.wait_ge(st2_ready, GB)
                            aggregate_group(0)
                        if c == 2:
                            sign(1)
                            signs_out(0)
                            signs_out(1)
                        if c == 5:
                            signs_out(2)
                        if c == 6:
                            apply_group(0)
                            low_group(0)
                        if c == 7:
                            signs_out(3)
                            tokens_out(0, 0, True)
                            tokens_out(0, 1, True)
                if tt in (-1, 0, 1):
                    offsets(tt + 2)
                if tt in (-2, -1, 0):
                    statistics(tt + 3)
                if tt == -2:
                    largest_scale()
                if tt == 1:
                    output_factors()
            steps(dve, step)

            def group(n, first, more):
                for k in range(HK):
                    if more and k == 1:
                        dve.wait_ge(st2_ready, (n + 1) * GB + GB)
                    dve.wait_ge(hh_ready, n * HK + k + 1)
                    nc.vector.tensor_tensor(HP[k % 4][:, 1, :], HF[k % 2][:, :], HP[k % 4][:, 0, :],
                                            ALU.subtract).then_inc(hl_ready, 1)
                    if more:
                        if k == 0:
                            norm_group(n + 1)
                        if k == 1:
                            aggregate_group(n + 1)
                        if k == 3:
                            apply_group(n + 1)
                        if k == 5:
                            low_group(n + 1)
                        if k >= 6:
                            tokens_out(n + 1, k - 6, False)
                if first:
                    dve.wait_ge(cs_ready, 1)
                for i in range(GB + 1):
                    if i < GB:
                        dve.wait_ge(y_done, n * GB + i + 1)
                        nc.vector.tensor_tensor(YS[:, i, :], YB[i][:, 0:E], CS[:, :], ALU.mult).then_inc(ys_ready, 1)
                    if i:
                        dve.wait_ge(ys_ready, n * GB + i)
                        xi = tokens_at(n, i - 1)
                        nc.vector.tensor_tensor(xi, xi, YS[:, i - 1, :], ALU.add).then_inc(y_ready, 1)

            group(0, True, True)
            with dve.Fori(1, NG - 1) as n:
                group(n, False, True)
            group(NG - 1, False, False)

        @block.tensor
        def _(pe):
            pe.wait_ge(ident, 2)
            pe.wait_ge(k_lo, 2)
            for i in range(B // 2):
                if i >= 4:
                    pe.wait_ge(k_ev[i % 2], (i - 4) // 2 + 1)
                for a in range(2 * JP):
                    g0 = (2 * i * KVH) + 2 * a
                    last = nc.tensor.transpose(KBANK[i % 4][:, a * 128:(a + 1) * 128],
                                               KP[:, g0:g0 + 2, :, :].rearrange("p j o c -> p (j o c)"), IDB[:, :])
                last.then_inc(k_tr, 1)

            def stack(b, r):
                pe.wait_ge(lo_ready, b + 1)
                for a in range(2):
                    for g in range(G):
                        h0 = 2 * ((2 * r + a) * G + g)
                        last = nc.tensor.transpose(
                            PQh[:, (a * G + g) * 128:(a * G + g + 1) * 128],
                            QS[:, h0:h0 + 2, :, :].rearrange("p h c r -> p (h c r)"), IDH[:, :])
                last.then_inc(qtr_done, 1)

            def scores(b, c, par):
                rows = slice(64 * (c % 2), 64 * (c % 2) + 64)
                for g in range(G):
                    last = nc.tensor.matmul(PS_[c % 2][:, g * 128:(g + 1) * 128],
                                            QT[par][rows, c // 2, g * 128:(g + 1) * 128],
                                            KTS[par][rows, c // 2, :], start=True, stop=True)
                last.then_inc(s_done, 1)

            def shifted(b, c, par):
                rows = slice(64 * (c % 2), 64 * (c % 2) + 64)
                nc.tensor.matmul(PT_[c % 2][:, :], KTT[par][rows, c // 2, :], QT[par][rows, c // 2, :],
                                 start=True, stop=True).then_inc(t_done, 1)

            def sums(b, hf, par):
                for c in range(4):
                    last = nc.tensor.matmul(PO[32 * c:32 * c + 32, :], V[par][:, 4 * hf + c, :],
                                            P[par][:, 4 * hf + c, :], start=True, stop=True)
                last.then_inc(pv_done, 1)

            def queries_back(b, hf):
                pe.wait_ge(os_ready, 2 * b + hf + 1)
                for g in range(G):
                    last = nc.tensor.transpose(PX[:, g * 128:(g + 1) * 128], OS[hf][:, g * 128:(g + 1) * 128], IDF[:, :])
                last.then_inc(otr_done, 1)

            def shift_back(b, hf):
                pe.wait_ge(mp_ready, 2 * b + hf + 1)
                nc.tensor.transpose(PMh[0:32, 0:128], MP[:, :, :, :, :].rearrange("p a b c g -> p (a b c g)"),
                                    IDH[:, :]).then_inc(mtr_done, 1)

            def signs(i):
                pe.wait_ge(sign_done, 1 if i < FC else 2)
                if i == 3:
                    pe.wait_ge(wt_ready, 1)
                for a in range(8):
                    if i < FC:
                        src = SU[:, a, i * 128:(i + 1) * 128]
                    else:
                        k, c = 4 * (i - FC) + a // FC, a % FC
                        src = SD[:, c, k * 128:(k + 1) * 128]
                    last = nc.tensor.transpose(SBANK[i][:, a * 128:(a + 1) * 128], src, IDH[:, :])
                last.then_inc(wtr_done, 1)

            def tokens(n, p, first):
                if p == 0:
                    pe.wait_ge(xh_ready, n + 1)
                    if first:
                        pe.wait_ge(wt_ready, 3)
                    else:
                        pe.wait_ge(xt_ready, 2 * n)
                else:
                    pe.wait_ge(xl_ready, n + 1)
                    pe.wait_ge(xt_ready, 2 * n + 1)
                for c in range(FC):
                    for i in range(GB):
                        a = c * GB + i
                        last = nc.tensor.transpose(PQh[:, a * 128:(a + 1) * 128],
                                                   XH[:, p, i, c * 128:(c + 1) * 128], IDH[:, :])
                last.then_inc(xtr_done, 1)

            def up(n, k, first):
                if k == 0:
                    pe.wait_ge(xt_ready, 2 * n + 2)
                    if first:
                        pe.wait_ge(mt_ready, 2 * B)
                        pe.wait_ge(wt_ready, 4)
                if k >= 3:
                    pe.wait_ge(hh_ready, n * HK + k - 2)
                elif not first:
                    pe.wait_ge(hh_ready, n * HK + (-1, 0, -2)[k])
                for p in range(2):
                    for c in range(FC):
                        last = nc.tensor.matmul(UPB[k % 3][:, :], UT[:, c, k * 128:(k + 1) * 128], XT[:, p, c, :],
                                                start=(p == 0 and c == 0), stop=(p == 1 and c == FC - 1))
                last.then_inc(up_done, 1)

            def step(t, par, tt):
                nxt = 1 - par
                if has(tt, 1):
                    pe.wait_ge(kts_ld[nxt], 16 * turn(t, par, 1))
                    pe.wait_ge(qt_ready[0], t + 2)
                    if tt != -1:
                        pe.wait_ge(max_done, NC * (t + 1) - 1)
                    scores(t + 1, 0, nxt)
                for c in range(NC):
                    if has(tt, 1) and c + 1 < NC:
                        if c + 1 == 4:
                            pe.wait_ge(qt_ready[1], t + 2)
                        if tt != -1 or c >= 1:
                            pe.wait_ge(max_done, NC * (t + 1) + c)
                        scores(t + 1, c + 1, nxt)
                    if has(tt, 0):
                        if c == 0:
                            pe.wait_ge(ktt_ld[par], 16 * turn(t, par, 0))
                            pe.wait_ge(m_ld[0], 16 * (t + 1))
                        if c == 4:
                            pe.wait_ge(m_ld[1], 16 * (t + 1))
                        if tt != 0 or c >= 2:
                            pe.wait_ge(exp_done, NC * t + c - 1)
                        shifted(t, c, par)
                    if c == 0 and has(tt, 0):
                        pe.wait_ge(mt_ready, 2 * t + 1)
                        shift_back(t, 1)
                    if c == 0 and has(tt, 1):
                        pe.wait_ge(qt_ready[0], t + 2)
                        stack(t + 1, 1)
                    if c == 2 and has(tt, -1):
                        if tt != 1:
                            pe.wait_ge(ao_ready, 2 * t - 2)
                        queries_back(t - 1, 0)
                    if c == 1:
                        if has(tt, -1):
                            pe.wait_ge(exp_done, NC * t)
                            pe.wait_ge(os_ready, 2 * t - 1)
                            sums(t - 1, 1, nxt)
                    if c == 6 and has(tt, -1):
                        pe.wait_ge(ao_ready, 2 * t - 1)
                        queries_back(t - 1, 1)
                    if c == 5 and has(tt, 0):
                        pe.wait_ge(v_ld[par], 16 * turn(t, par, 0))
                        pe.wait_ge(exp_done, NC * t + 4)
                        if tt != 0:
                            pe.wait_ge(os_ready, 2 * t)
                        sums(t, 0, par)
                    if c == 4 and has(tt, 1):
                        if tt == -1:
                            for i in range(2):
                                pe.wait_ge(k_ev[i], B // 4)
                        else:
                            pe.wait_ge(mt_ready, 2 * (t + 1))
                        shift_back(t + 1, 0)
                    if c == 4 and has(tt, 2):
                        if tt == -2:
                            pe.wait_ge(k_ev[0], B // 4 - 1)
                        else:
                            pe.wait_ge(qt_ready[1], t + 2)
                        stack(t + 2, 0)
                    if tt == B - 1:
                        if c == 2:
                            pe.wait_ge(max_done, NC * B)
                            signs(0)
                            signs(1)
                        if c == 3:
                            signs(2)
                        if c == 5:
                            signs(3)
                        if c == 7:
                            tokens(0, 0, True)
                            tokens(0, 1, True)
                    if tt == B and c == 2:
                        up(0, 0, True)
                        up(0, 1, True)
            steps(pe, step)

            def down(n, k, first):
                pe.wait_ge(hl_ready, n * HK + k + 1)
                for i in range(GB):
                    if k == 0:
                        if not first:
                            pe.wait_ge(ys_ready, n * GB + i - GB + 1)
                        elif i == 0:
                            pe.wait_ge(exp_done, NC * B)
                            pe.wait_ge(os_ready, 2 * B)
                            pe.wait_ge(ao_ready, 2 * B)
                    for p in range(2):
                        last = nc.tensor.matmul(YB[i][:, 0:E], HP[k % 4][:, p, i * 128:(i + 1) * 128], DT[:, k, :],
                                                start=(k == 0 and p == 0), stop=(k == HK - 1 and p == 1))
                    if k == HK - 1:
                        last.then_inc(y_done, 1)
                if k < HK - 1:
                    last.then_inc(down_done, 1)

            def group(n, first, more):
                for k in range(HK + 2):
                    if k < HK and not (first and k < 2):
                        up(n, k, first)
                    if k >= 2:
                        if more and k >= HK:
                            tokens(n + 1, k - HK, False)
                        down(n, k - 2, first)

            group(0, True, True)
            with pe.Fori(1, NG - 1) as n:
                group(n, False, True)
            group(NG - 1, False, False)


_INS = ['x', 'ctx_512', 'g_xattn', 'g_ffn', 'L0_ffn_up_weight', 'L0_ffn_down_weight', 'L0_ffn_up_scale',
        'L0_ffn_down_scale', 'L0_ffn_output_scale']


def kernel(**inputs):
    import numpy as _np
    import concourse.bacc as _bacc
    from concourse import mybir as _mybir
    from concourse.bass_utils import run_bass_kernel_spmd as _run

    nc = _bacc.Bacc("TRN2", target_bir_lowering=False, num_devices=1)
    arrays, args = {}, []
    for name in _INS:
        a = _np.ascontiguousarray(inputs[name])
        arrays[f"in_{name}"] = a
        args.append(nc.dram_tensor(f"in_{name}", a.shape, _mybir.dt.from_np(a.dtype), kind="ExternalInput").ap())
    args.append(nc.dram_tensor("out_0", inputs['x'].shape, _mybir.dt.float32, kind="ExternalOutput").ap())
    flamingo_kernel(nc, *args)
    r = _run(nc, [arrays], core_ids=[0])
    return r.results[0]["out_0"]
```

```python
import concourse.bass as bass
from concourse import mybir
from contextlib import ExitStack


def flamingo_kernel(nc: bass.Bass, x, ctx_in, g_xattn, g_ffn, up_w, down_w, up_s, down_s, out_s, out):
    fp32, bf16, fp16 = mybir.dt.float32, mybir.dt.bfloat16, mybir.dt.float16
    ALU, ACT, AX = mybir.AluOpType, mybir.ActivationFunctionType, mybir.AxisListType

    B, S, E = x.shape
    KF = ctx_in.shape[2]
    D = 8
    KVH = KF // D
    QH = E // D
    G = QH // KVH
    JP = KVH // 2
    HID = up_w.shape[0]
    HK = HID // 128
    FC = E // 128
    GB = 4
    NG = B // GB
    EPS = 1e-5
    SCALE = float(D) ** -0.5
    SHIFT = float(2 ** 20)
    UP_TARGET = 64.0
    ONE = 3 * D
    NC = KVH
    PIPE = 2

    es = ExitStack()
    with es:
        def sb(name, shape, dt):
            return es.enter_context(nc.sbuf_tensor(name, shape, dt))

        def pb(name, shape, dt):
            return es.enter_context(nc.psum_tensor(name, shape, dt))

        def sem(name):
            return es.enter_context(nc.semaphore(name))

        X = sb("X", [128, B, E], fp32)
        CTX = sb("CTX", [128, B, KF], fp32)
        KP = sb("KP", [128, B * KVH, 2, 32], bf16)
        KR = sb("KR", [128, B * KVH, D], fp32)
        KTA = sb("KTA", [128, B, JP * 128], bf16)
        KTS = [sb(f"KTS{i}", [128, JP, 128], bf16) for i in range(2)]
        KTT = [sb(f"KTT{i}", [128, JP, 128], bf16) for i in range(2)]
        VA = sb("VA", [128, B, KVH * 32], fp32)
        V = [sb(f"V{i}", [128, KVH, 32], fp32) for i in range(2)]
        Q = sb("Q", [128, QH, D], fp32)
        QS = sb("QS", [128, QH, 2, 32], fp16)
        QT = [sb(f"QT{i}", [128, JP, G * 128], fp16) for i in range(2)]
        NM = [sb(f"NM{i}", [128, 2, 2, 2, G], fp32) for i in range(2)]
        MP = sb("MP", [128, 2, 2, 2, G], fp16)
        MT = [sb(f"MT{i}", [32, 128], fp16) for i in range(2)]
        P = [sb(f"P{i}", [128, KVH, G * 128], fp32) for i in range(2)]
        OS = [sb(f"OS{i}", [128, G * 128], fp32) for i in range(2)]
        RC = [sb(f"RC{i}", [128, G, 4], fp32) for i in range(2)]
        AO = [sb(f"AO{i}", [128, 2, 4, G, D], fp32) for i in range(2)]
        ST1 = sb("ST1", [128, B, 6], fp32)
        MV1 = sb("MV1", [128, B, 2], fp32)
        VE1 = sb("VE1", [128, B], fp32)
        RS1 = sb("RS1", [128, B], fp32)
        NB1 = sb("NB1", [128, B], fp32)
        HALF = sb("HALF", [128, B], fp32)
        IDF = sb("IDF", [128, 128], fp32)
        IDH = sb("IDH", [128, 128], fp16)
        IDB = sb("IDB", [128, 128], bf16)
        GX = sb("GX", [128, 1], fp32)
        TX = sb("TX", [128, 1], fp32)
        GF = sb("GF", [128, 1], fp32)
        TF = sb("TF", [128, 1], fp32)
        OSC = sb("OSC", [128, 1], fp32)
        DS = sb("DS", [128, E], fp32)
        CS = sb("CS", [128, E], fp32)
        US = sb("US", [128, HK], fp32)
        UN = sb("UN", [128, HK], fp32)
        um = sb("um", [128, 1], fp32)
        uma = sb("uma", [128, 1], fp32)
        umg = sb("umg", [128, 1], fp32)
        umr = sb("umr", [128, 1], fp32)
        fac = sb("fac", [128, 1], fp32)
        UW = sb("UW", [128, HK, E], fp32)
        DW = sb("DW", [128, FC, HID], fp32)
        SU = sb("SU", [128, HK, E], fp16)
        SD = sb("SD", [128, FC, HID], fp16)
        UT = sb("UT", [128, FC, HID], fp16)
        DT = sb("DT", [128, HK, E], fp16)
        WF = [w[:, :, :].rearrange("p a b -> p (a b)") for w in (UW, DW)]
        WS = [w[:, :, :].rearrange("p a b -> p (a b)") for w in (SU, SD)]
        ST2 = sb("ST2", [128, GB, 6], fp32)
        MV2 = sb("MV2", [128, GB, 2], fp32)
        VE2 = sb("VE2", [128, GB], fp32)
        RS2 = sb("RS2", [128, GB], fp32)
        XN = sb("XN", [128, GB, E], fp32)
        XH = sb("XH", [128, 2, GB, E], fp16)
        XT = sb("XT", [128, 2, FC, GB * 128], fp16)
        HF = [sb(f"HF{i}", [128, 512], fp32) for i in range(2)]
        HP = [sb(f"HP{i}", [128, 2, 512], fp16) for i in range(4)]
        YS = sb("YS", [128, GB, E], fp32)

        PS_ = [pb(f"PS{i}", [128, 512], fp32) for i in range(2)]
        PT_ = [pb(f"PT{i}", [128, 512], fp32) for i in range(2)]
        PQ = pb("PQ", [128, 512], fp32)
        PM = pb("PM", [128, 512], fp32)
        PO = pb("PO", [128, 512], fp32)
        PX = pb("PX", [128, 512], fp32)
        PQh, PMh = PQ[:, :].bitcast(fp16), PM[:, :].bitcast(fp16)
        KBANK = [b[:, :].bitcast(bf16) for b in (PQ, PM, PO, PX, PT_[0], PT_[1], PO, PX)]
        K_DVE = (0, 7)
        K_ACT = tuple(i for i in range(B // 2) if i not in K_DVE)
        SBANK = [b[:, :].bitcast(fp16) for b in (PO, PX, PQ, PS_[0])]
        UPB = [PS_[0], PS_[1], PM]
        YB = [PT_[0], PT_[1], PO, PX]

        ld_ctx = [sem(f"ld_ctx{i}") for i in range(2)]
        ld_x = [sem(f"ld_x{i}") for i in range(NG)]
        ld_small = sem("ld_small")
        ld_g = sem("ld_g")
        ld_w = [sem(f"ld_w{i}") for i in range(2)]
        ident = sem("ident")
        zeroed = sem("zeroed")
        k_hi, k_r1, k_mid0, k_mid, k_lo, k_twice = (
            sem(n) for n in ("k_hi", "k_r1", "k_mid0", "k_mid", "k_lo", "k_twice"))
        v_ready = sem("v_ready")
        k_tr, k_ev_dve, k_ev_act = sem("k_tr"), sem("k_ev_dve"), sem("k_ev_act")
        st_ready, mv_ready, ve_ready, rs_ready, nb_ready = (
            sem(n) for n in ("st_ready", "mv_ready", "ve_ready", "rs_ready", "nb_ready"))
        tx_ready = sem("tx_ready")
        q_ready, hi_ready, lo_ready = sem("q_ready"), sem("hi_ready"), sem("lo_ready")
        qtr_done, qt_ready = sem("qtr_done"), [sem(f"qt_ready{i}") for i in range(2)]
        kts_ld = [sem(f"kts_ld{i}") for i in range(2)]
        ktt_ld = [sem(f"ktt_ld{i}") for i in range(2)]
        v_ld = [sem(f"v_ld{i}") for i in range(2)]
        s_done, max_done = sem("s_done"), sem("max_done")
        mh_ready, mp_ready, mtr_done, mt_ready = sem("mh_ready"), sem("mp_ready"), sem("mtr_done"), sem("mt_ready")
        m_ld = [sem(f"m_ld{i}") for i in range(2)]
        t_done, exp_done = sem("t_done"), sem("exp_done")
        pv_done, os_ready, otr_done = sem("pv_done"), sem("os_ready"), sem("otr_done")
        rc_ready, ao_ready, x1_ready = sem("rc_ready"), sem("ao_ready"), sem("x1_ready")
        sign_done, wtr_done, wt_act, wt_dve = (sem(n) for n in ("sign_done", "wtr_done", "wt_act", "wt_dve"))
        um_ready, uma_ready, us_step, un_ready, cs_ready = (
            sem(n) for n in ("um_ready", "uma_ready", "us_step", "un_ready", "cs_ready"))
        st2_ready, mv2_ready, ve2_ready, rs2_ready, xn_ready, xh_ready, xl_ready = (
            sem(n) for n in ("st2_ready", "mv2_ready", "ve2_ready", "rs2_ready", "xn_ready", "xh_ready", "xl_ready"))
        xtr_done, xt_ready = sem("xtr_done"), sem("xt_ready")
        up_done, hf_ready, hh_ready, hl_ready, down_done, y_done = (
            sem(n) for n in ("up_done", "hf_ready", "hh_ready", "hl_ready", "down_done", "y_done"))
        ys_ready, y_ready, stored = sem("ys_ready"), sem("y_ready"), sem("stored")

        block = es.enter_context(nc.Block())

        HEAD, TAIL = (-2, -1, 0, 1), (B - 2, B - 1, B)
        LOOP = (2, B - 2)

        def steps(engine, step):
            for t in HEAD:
                step(t, t % 2, t)
            with engine.Fori(0, (LOOP[1] - LOOP[0]) // PIPE) as i:
                for u in range(PIPE):
                    step(i * PIPE + LOOP[0] + u, (LOOP[0] + u) % 2, None)
            for t in TAIL:
                step(t, t % 2, t)

        STAT = (slice(0, 1), slice(1, GB)) + tuple(slice(n * GB, n * GB + GB) for n in range(1, NG))

        KROWS = (slice(0, GB * KVH), slice(GB * KVH, B * KVH))

        def keys_left(engine, i):
            if i in K_DVE:
                engine.wait_ge(k_ev_dve, K_DVE.index(i) + 1)
            else:
                engine.wait_ge(k_ev_act, K_ACT.index(i) + 1)

        def has(t, d):
            return t is None or 0 <= t + d < B

        def turn(t, par, d):
            odd = (par + d) % 2
            return (t + d - odd) // 2 + 1 if isinstance(t, int) else (t + (d - odd)) // 2 + 1

        @block.sync
        def _(sp):
            def load_context(i):
                bs = (slice(0, GB), slice(GB, B))[i]
                sp.dma_start(CTX[:, bs, :], ctx_in[bs, :, :].rearrange("b s f -> s b f")).then_inc(ld_ctx[i], 16)

            def load_tokens(n):
                sp.dma_start(X[:, n * GB:(n + 1) * GB, :],
                             x[n * GB:(n + 1) * GB, :, :].rearrange("b s f -> s b f")).then_inc(ld_x[n], 16)

            load_context(0)
            load_tokens(0)
            load_context(1)
            load_tokens(1)

            def later_loads():
                sp.dma_start(UW[:, :, :], up_w.rearrange("(k p) f -> p k f", p=128)).then_inc(ld_w[0], 16)
                for n in range(2, NG):
                    load_tokens(n)
                sp.dma_start(DW[:, :, :], down_w.rearrange("(c p) h -> p c h", p=128)).then_inc(ld_w[1], 16)

            def shift_rows(b, hf, par):
                sp.dma_start(QT[par][ONE:128:32, 2 * hf:2 * hf + 2, :], MT[hf][:, :]).then_inc(m_ld[hf], 16)

            def step(t, par, tt):
                nxt = 1 - par
                if has(tt, 2):
                    if tt is None or tt >= 0:
                        sp.wait_ge(s_done, NC * (t + 1))
                    if tt is not None and tt % 2 == 0 and tt < LOOP[0]:
                        keys_left(sp, (tt + 2) // 2)
                    sp.dma_start(KTS[par][:, :, :], KTA[:, bass.ds(t + 2, 1), :].rearrange(
                        "p o (j t) -> p (o j) t", j=JP)).then_inc(kts_ld[par], 16)
                if has(tt, 1):
                    if tt is None or tt >= 1:
                        sp.wait_ge(t_done, NC * t)
                    sp.dma_start(KTT[nxt][:, :, :], KTA[:, bass.ds(t + 1, 1), :].rearrange(
                        "p o (j t) -> p (o j) t", j=JP)).then_inc(ktt_ld[nxt], 16)
                if tt == -1:
                    later_loads()
                if has(tt, 0):
                    sp.wait_ge(mt_ready, 2 * t + 2)
                    shift_rows(t, 1, par)
                if has(tt, 1):
                    if tt == -1:
                        sp.wait_ge(v_ready, 3)
                    if tt is None or tt >= 1:
                        sp.wait_ge(pv_done, 2 * t)
                    sp.dma_start(V[nxt][:, :, :], VA[:, bass.ds(t + 1, 1), :].rearrange(
                        "p o (j c) -> p (o j) c", j=KVH)).then_inc(v_ld[nxt], 16)
                    sp.wait_ge(mt_ready, 2 * (t + 1) + 1)
                    shift_rows(t + 1, 0, nxt)
                if tt == HEAD[-1]:
                    sp.wait_ge(k_ev_dve, len(K_DVE))
                    sp.wait_ge(k_ev_act, len(K_ACT))
            steps(sp, step)

            for n in range(NG):
                for i in range(GB):
                    sp.wait_ge(y_ready, n * GB + i + 1)
                    sp.dma_start(out[n * GB + i, :, :], X[:, n * GB + i, :]).then_inc(stored, 16)
            sp.wait_ge(stored, 16 * B)

        @block.gpsimd
        def _(pool):
            nc.gpsimd.memset(IDF[:, :], 0.0).then_inc(zeroed, 1)
            pool.wait_ge(zeroed, 1)
            nc.gpsimd.affine_select(out=IDF[:, :], in_=IDF[:, :], compare_op=ALU.not_equal, fill=1.0, base=0,
                                    pattern=[[-1, 128]], channel_multiplier=1).then_inc(ident, 1)
            nc.gpsimd.memset(HALF[:, :], -0.5).then_inc(x1_ready, 1)
            va = VA[:, :, :].rearrange("p b (j c) -> p (b j) c", c=32)
            nc.gpsimd.memset(va[:, :, D:D + 1], 1.0).then_inc(v_ready, 1)
            nc.gpsimd.memset(va[:, :, D + 1:32], 0.0).then_inc(v_ready, 1)

            def inverse_roots(n):
                pool.wait_ge(x1_ready, 1)
                pool.wait_ge(ve_ready, n + 1)
                nc.gpsimd.tensor_tensor(RS1[:, STAT[n]], VE1[:, STAT[n]], HALF[:, STAT[n]],
                                        ALU.pow).then_inc(rs_ready, 1)

            def step(t, par, tt):
                if tt == -2:
                    inverse_roots(0)
                if has(tt, 2):
                    pool.wait_ge(hi_ready, t + 3)
                    nc.gpsimd.tensor_tensor(
                        QS[:, :, 1, 0:ONE].rearrange("p h (r d) -> p h r d", d=D),
                        Q[:, :, :].rearrange("p h (o d) -> p h o d", o=1).to_broadcast([128, QH, 3, D]),
                        QS[:, :, 0, 0:ONE].rearrange("p h (r d) -> p h r d", d=D),
                        ALU.subtract).then_inc(lo_ready, 1)
                if tt in HEAD:
                    inverse_roots(tt + 3)
                if tt == B - 2:
                    pool.wait_ge(ve2_ready, 1)
                    nc.gpsimd.tensor_tensor(RS2[:, :], VE2[:, :], HALF[:, 0:GB], ALU.pow).then_inc(rs2_ready, 1)
                if has(tt, -1):
                    pool.wait_ge(ao_ready, 2 * t)
                    xb = X[:, bass.ds(t - 1, 1), :].rearrange("p o f -> p (o f)")
                    nc.gpsimd.tensor_tensor(xb, xb, AO[1 - par][:, :, :, :, :].rearrange("p h c g d -> p (h c g d)"),
                                            ALU.add).then_inc(x1_ready, 1)
                if tt == 0:
                    pool.wait_ge(um_ready, 1)
                    nc.gpsimd.partition_all_reduce(uma[:, :], um[:, :], 128,
                                                   bass.bass_isa.ReduceOp.max).then_inc(uma_ready, 1)
            steps(pool, step)

            with pool.Fori(0, NG - 1) as n:
                pool.wait_ge(ve2_ready, n + 2)
                nc.gpsimd.tensor_tensor(RS2[:, :], VE2[:, :], HALF[:, 0:GB], ALU.pow).then_inc(rs2_ready, 1)

        @block.scalar
        def _(act):
            act.dma_start(GX[:, :], g_xattn[None, :].to_broadcast([128, 1])).then_inc(ld_g, 16)
            act.dma_start(GF[:, :], g_ffn[None, :].to_broadcast([128, 1])).then_inc(ld_g, 16)
            act.dma_start(OSC[:, :], out_s[None, :].to_broadcast([128, 1])).then_inc(ld_small, 16)
            act.dma_start(DS[:, :], down_s[None, :].to_broadcast([128, E])).then_inc(ld_small, 16)
            act.dma_start(US[:, :], up_s.rearrange("(k p) -> p k", p=128),
                          allow_slow_non_contiguous=True).then_inc(ld_small, 16)
            def middle():
                act.wait_ge(k_r1, 2)
                nc.scalar.copy(KP[:, KROWS[1], 0, D:2 * D], KR[:, KROWS[1], :]).then_inc(k_mid, 1)

            def values():
                act.wait_ge(ld_ctx[0], 16)
                act.wait_ge(ld_ctx[1], 16)
                act.wait_ge(tx_ready, 1)
                nc.scalar.mul(VA[:, :, :].rearrange("p b (j c) -> p (b j) c", c=32)[:, :, 0:D],
                              CTX[:, :, :].rearrange("p b (j d) -> p (b j) d", d=D), TX[:, 0:1]).then_inc(v_ready, 1)

            def keys_out(i):
                act.wait_ge(k_tr, i + 1)
                nc.scalar.copy(KTA[:, 2 * i:2 * i + 2, :].rearrange("p b n -> p (b n)"),
                               KBANK[i][:, 0:1024]).then_inc(k_ev_act, 1)

            def sign(n, quarter):
                act.wait_ge(ld_w[n], 16)
                w = slice(quarter * HK * E // 4, (quarter + 1) * HK * E // 4)
                nc.scalar.activation(WS[n][:, w], WF[n][:, w], ACT.Sign).then_inc(sign_done, 1)

            act.wait_ge(ld_g, 32)
            nc.scalar.activation(TX[:, :], GX[:, :], ACT.Tanh).then_inc(tx_ready, 1)
            nc.scalar.activation(TF[:, :], GF[:, :], ACT.Tanh).then_inc(tx_ready, 1)

            def hidden(n, k, first, more):
                act.wait_ge(up_done, n * HK + k + 1)
                if k >= 2 or not first:
                    act.wait_ge(hl_ready, n * HK + k - 1)
                nc.scalar.activation(HF[k % 2][:, :], UPB[k % 3][:, :], ACT.Relu,
                                     scale=UN[:, k:k + 1]).then_inc(hf_ready, 1)
                if k >= 4:
                    act.wait_ge(down_done, n * (HK - 1) + k - 3)
                elif k == 3 and not first:
                    act.wait_ge(y_done, n * GB)
                elif not first:
                    act.wait_ge(down_done, n * (HK - 1) + k - 2)
                nc.scalar.activation(HP[k % 4][:, 0, :], UPB[k % 3][:, :], ACT.Relu,
                                     scale=UN[:, k:k + 1]).then_inc(hh_ready, 1)
                if k == 4 and more:
                    act.wait_ge(xn_ready, n + 2)
                    act.wait_ge(xtr_done, 2 * n + 2)
                    nc.scalar.copy(XH[:, 0, :, :], XN[:, :, :]).then_inc(xh_ready, 1)

            def layer_norm(b):
                for side in range(2):
                    nc.scalar.activation(
                        Q[:, :, :].rearrange("p (j g s) d -> p j g s d", j=JP, s=2)[:, :, :, side, :],
                        X[:, bass.ds(b, 1), :].rearrange(
                            "p o (j s g d) -> p (o j) s g d", j=JP, s=2, d=D)[:, :, side, :, :],
                        ACT.Identity, bias=NB1[:, bass.ds(b, 1)],
                        scale=RS1[:, bass.ds(b, 1)]).then_inc(q_ready, 1)

            def step(t, par, tt):
                if has(tt, 2):
                    if tt in HEAD:
                        act.wait_ge(nb_ready, 1 if tt == -2 else 2)
                    if tt is None or tt >= -1:
                        act.wait_ge(lo_ready, t + 2)
                    layer_norm(t + 2)
                for c in range(NC):
                    if has(tt, 0):
                        act.wait_ge(t_done, NC * t + c + 1)
                        if tt is None or tt >= 2:
                            if c % 4 == 0:
                                act.wait_ge(pv_done, 2 * (t - 2) + c // 4 + 1)
                        nc.scalar.activation(P[par][:, c, :], PT_[c % 2][:, :], ACT.Exp,
                                             scale=SCALE).then_inc(exp_done, 1)
                    if c == 0 and has(tt, 2):
                        act.wait_ge(q_ready, 2 * (t + 3))
                        if tt != -2:
                            act.wait_ge(qtr_done, 2 * (t + 2))
                        nc.scalar.copy(QS[:, :, 0, 0:ONE].rearrange("p h (r d) -> p h r d", d=D),
                                       Q[:, :, :].rearrange("p h (o d) -> p h o d", o=1).to_broadcast(
                                           [128, QH, 3, D])).then_inc(hi_ready, 1)
                    if tt == -2:
                        if c == 1:
                            middle()
                            values()
                        if c == 2:
                            keys_out(1)
                    if tt == -1:
                        if c == 1:
                            keys_out(3)
                        if c == 3:
                            keys_out(4)
                            sign(0, 0)
                            sign(0, 1)
                        if c == 6:
                            keys_out(5)
                            sign(0, 2)
                            sign(0, 3)
                            keys_out(6)
                    if tt == 0 and c == 3:
                        act.wait_ge(wtr_done, 1)
                        nc.scalar.copy(UT[:, 0, :], SBANK[0][:, 0:1024]).then_inc(wt_act, 1)
                    if c == 2 and has(tt, -1):
                        act.wait_ge(pv_done, 2 * t)
                        if tt != 1:
                            act.wait_ge(otr_done, 2 * t - 2)
                        nc.scalar.copy(OS[1][:, :], PO[:, :]).then_inc(os_ready, 1)
                    if tt in (0, 1) and c in (1, 4):
                        sign(1, 2 * tt + c // 4)
                    if tt == B - 2 and c == 1:
                        act.wait_ge(qtr_done, 2 * B)
                        act.wait_ge(t_done, NC * (B - 2))
                        nc.scalar.copy(QT[(B - 1) % 2][:, 2:4, :].rearrange("p a n -> p (a n)"),
                                       PQh[:, 0:1024]).then_inc(qt_ready[1], 1)
                    if tt == B - 1:
                        if c < 2:
                            act.wait_ge(xn_ready, 1)
                            high = nc.scalar.copy(XH[:, 0, 2 * c:2 * c + 2, :], XN[:, 2 * c:2 * c + 2, :])
                            if c == 1:
                                high.then_inc(xh_ready, 1)
                        if c == 7:
                            act.wait_ge(un_ready, 1)
                            hidden(0, 0, True, True)
                    if tt == B and c == 2:
                        hidden(0, 1, True, True)
                    if tt == -2 and c == 3:
                        keys_out(2)
                    if c == 4 and has(tt, 2) and tt != -2:
                        act.wait_ge(qtr_done, 2 * (t + 2) + 1)
                        if tt is None or tt >= 0:
                            act.wait_ge(t_done, NC * t + 4)
                        nc.scalar.copy(QT[par][:, 0:2, :].rearrange("p a n -> p (a n)"),
                                       PQh[:, 0:1024]).then_inc(qt_ready[0], 1)
                    if c == 5 and has(tt, 0):
                        act.wait_ge(pv_done, 2 * t + 1)
                        if tt is None or tt >= 1:
                            act.wait_ge(otr_done, 2 * t - 1)
                        nc.scalar.copy(OS[0][:, :], PO[:, :]).then_inc(os_ready, 1)
                if tt == HEAD[-1]:
                    act.wait_ge(nb_ready, len(STAT))
            steps(act, step)

            for k in range(2, HK):
                hidden(0, k, True, True)
            with act.Fori(1, NG - 1) as n:
                for k in range(HK):
                    hidden(n, k, False, True)
            for k in range(HK):
                hidden(NG - 1, k, False, False)

        @block.vector
        def _(dve):
            CX = CTX[:, :, :].rearrange("p b (j d) -> p (b j) d", d=D)
            nc.vector.memset(KP[:, :, 0, ONE + 1:32], 0.0)
            nc.vector.memset(KP[:, :, 0, ONE:ONE + 1], SHIFT)
            nc.vector.memset(QS[:, :, :, ONE:32], 0.0)
            dve.wait_ge(ident, 1)
            nc.vector.tensor_copy(IDH[:, :], IDF[:, :])
            nc.vector.tensor_copy(IDB[:, :], IDF[:, :]).then_inc(ident, 1)

            def high_rest(i):
                ks = KROWS[i]
                dve.wait_ge(ld_ctx[i], 16)
                nc.vector.tensor_copy(KP[:, ks, 0, 0:D], CX[:, ks, :]).then_inc(k_hi, 1)
                if i:
                    offsets(0)
                dve.wait_ge(k_hi, i + 1)
                nc.vector.tensor_tensor(KR[:, ks, :], CX[:, ks, :], KP[:, ks, 0, 0:D], ALU.subtract).then_inc(k_r1, 1)

            def low_twice(i):
                ks = KROWS[i]
                if i:
                    dve.wait_ge(k_mid, 1)
                else:
                    dve.wait_ge(k_r1, 1)
                    nc.vector.tensor_copy(KP[:, ks, 0, D:2 * D], KR[:, ks, :]).then_inc(k_mid0, 1)
                    dve.wait_ge(k_mid0, 1)
                nc.vector.tensor_tensor(KP[:, ks, 0, 2 * D:3 * D], KR[:, ks, :], KP[:, ks, 0, D:2 * D],
                                        ALU.subtract).then_inc(k_lo, 1)
                dve.wait_ge(k_lo, i + 1)
                nc.vector.tensor_copy(KP[:, ks, 1, :], KP[:, ks, 0, :]).then_inc(k_twice, 1)

            def keys_out(i):
                dve.wait_ge(k_tr, i + 1)
                nc.vector.tensor_copy(KTA[:, 2 * i:2 * i + 2, :].rearrange("p b n -> p (b n)"),
                                      KBANK[i][:, 0:1024]).then_inc(k_ev_dve, 1)

            def statistics(b):
                dve.wait_ge(ld_x[b // GB], 16)
                nc.vector.bn_stats(ST1[:, b, :], X[:, b, :]).then_inc(st_ready, 1)

            def aggregates(n):
                for b in range(STAT[n].start, STAT[n].stop):
                    dve.wait_ge(st_ready, b + 1)
                    nc.vector.bn_aggr(MV1[:, b, :], ST1[:, b, :]).then_inc(mv_ready, 1)
                dve.wait_ge(mv_ready, STAT[n].stop)
                nc.vector.tensor_scalar(VE1[:, STAT[n]], MV1[:, STAT[n], 1], EPS, None, ALU.add).then_inc(ve_ready, 1)

            def offsets(n):
                r = STAT[n]
                dve.wait_ge(rs_ready, n + 1)
                nc.vector.scalar_tensor_tensor(NB1[:, r], MV1[:, r, 0], -1.0, RS1[:, r], ALU.mult,
                                               ALU.mult).then_inc(nb_ready, 1)

            high_rest(0)
            low_twice(0)
            statistics(0)
            aggregates(0)
            keys_out(0)
            high_rest(1)
            for b in range(1, GB):
                statistics(b)
            aggregates(1)
            low_twice(1)
            offsets(1)
            for b in range(GB, 2 * GB - 1):
                statistics(b)

            def largest_scale():
                dve.wait_ge(ld_small, 48)
                nc.vector.tensor_reduce(um[:, :], US[:, :], AX.X, ALU.max,
                                        apply_absolute_value=True).then_inc(um_ready, 1)

            def output_factors():
                dve.wait_ge(uma_ready, 1)
                nc.vector.tensor_scalar(umg[:, :], uma[:, :], 1e-30, None, ALU.max).then_inc(us_step, 1)
                dve.wait_ge(us_step, 1)
                nc.vector.reciprocal(umr[:, :], umg[:, :]).then_inc(us_step, 1)
                dve.wait_ge(us_step, 2)
                nc.vector.tensor_scalar(UN[:, :], US[:, :], umr[:, 0:1], UP_TARGET, ALU.mult,
                                        ALU.mult).then_inc(un_ready, 1)
                dve.wait_ge(tx_ready, 2)
                nc.vector.tensor_scalar(fac[:, :], umg[:, :], TF[:, 0:1], 1.0 / UP_TARGET, ALU.mult,
                                        ALU.mult).then_inc(us_step, 1)
                dve.wait_ge(us_step, 3)
                nc.vector.tensor_scalar(CS[:, :], DS[:, :], OSC[:, 0:1], fac[:, 0:1], ALU.mult,
                                        ALU.mult).then_inc(cs_ready, 1)

            def signs_out(i):
                dve.wait_ge(wtr_done, i + 1)
                dst = UT[:, i, :] if i < FC else DT[:, 4 * (i - FC):4 * (i - FC) + 4, :].rearrange("p k n -> p (k n)")
                nc.vector.tensor_copy(dst, SBANK[i][:, 0:1024]).then_inc(wt_dve, 1)

            def tokens_at(n, i):
                return X[:, bass.ds(n * GB + i, 1), :].rearrange("p o f -> p (o f)")

            def norm_batch(n, i):
                nc.vector.bn_stats(ST2[:, i, :], tokens_at(n, i)).then_inc(st2_ready, 1)

            def norm_group(n):
                dve.wait_ge(x1_ready, n * GB + GB + 1)
                for i in range(GB):
                    norm_batch(n, i)

            def aggregate_group(n):
                for i in range(GB):
                    nc.vector.bn_aggr(MV2[:, i, :], ST2[:, i, :]).then_inc(mv2_ready, 1)
                dve.wait_ge(mv2_ready, n * GB + GB)
                nc.vector.tensor_scalar(VE2[:, :], MV2[:, :, 1], EPS, None, ALU.add).then_inc(ve2_ready, 1)

            def apply_group(n):
                dve.wait_ge(rs2_ready, n + 1)
                for i in range(GB):
                    last = nc.vector.tensor_scalar(XN[:, i, :], tokens_at(n, i), MV2[:, i, 0:1], RS2[:, i:i + 1],
                                                   ALU.subtract, ALU.mult)
                last.then_inc(xn_ready, 1)

            def low_group(n):
                dve.wait_ge(xh_ready, n + 1)
                nc.vector.tensor_tensor(XH[:, 1, :, :], XN[:, :, :], XH[:, 0, :, :], ALU.subtract).then_inc(xl_ready, 1)

            def tokens_out(n, p, first):
                dve.wait_ge(xtr_done, 2 * n + p + 1)
                if p == 0 and not first:
                    dve.wait_ge(up_done, HK * n)
                nc.vector.tensor_copy(XT[:, p, :, :].rearrange("p c n -> p (c n)"), PQh[:, 0:1024]).then_inc(xt_ready, 1)

            def hidden_low(n, k):
                dve.wait_ge(hh_ready, n * HK + k + 1)
                nc.vector.tensor_tensor(HP[k % 4][:, 1, :], HF[k % 2][:, :], HP[k % 4][:, 0, :],
                                        ALU.subtract).then_inc(hl_ready, 1)

            def maxima(t, c, par):
                dve.wait_ge(s_done, NC * t + c + 1)
                nc.vector.tensor_reduce(NM[par][:, c // 4, c % 2, c // 2 % 2, :], PS_[c % 2][:, :].rearrange(
                    "p (g t) -> p g t", g=G), AX.X, ALU.max, negate=True).then_inc(max_done, 1)

            def shift_high(b, hf, par, first):
                dve.wait_ge(max_done, NC * b + 4 * hf + 4)
                if not first:
                    dve.wait_ge(mtr_done, 2 * b + hf)
                nc.vector.tensor_scalar(MP[:, :, 0, :, :].rearrange("p s a g -> p s (a g)"),
                                        NM[par][:, hf, :, :, :].rearrange("p s a g -> p s (a g)"), 1.0 / SHIFT, None,
                                        ALU.mult).then_inc(mh_ready, 1)

            def shift_low(b, hf, par):
                dve.wait_ge(mh_ready, 2 * b + hf + 1)
                nc.vector.scalar_tensor_tensor(MP[:, :, 1, :, :].rearrange("p s a g -> p s (a g)"),
                                               NM[par][:, hf, :, :, :].rearrange("p s a g -> p s (a g)"), 1.0 / SHIFT,
                                               MP[:, :, 0, :, :].rearrange("p s a g -> p s (a g)"), ALU.mult,
                                               ALU.subtract).then_inc(mp_ready, 1)

            def shift_out(b, hf, first):
                dve.wait_ge(mtr_done, 2 * b + hf + 1)
                if not first:
                    dve.wait_ge(m_ld[hf], 16 * b)
                nc.vector.tensor_copy(MT[hf][:, :], PMh[0:32, 0:128]).then_inc(mt_ready, 1)

            def stacked_out(b, r, par, old):
                dve.wait_ge(qtr_done, 2 * b + r + 1)
                if old:
                    dve.wait_ge(t_done, NC * (b - 2) + 4 * r + 4)
                nc.vector.tensor_copy(QT[par][:, 2 * r:2 * r + 2, :].rearrange("p a n -> p (a n)"),
                                      PQh[:, 0:1024]).then_inc(qt_ready[r], 1)

            by_head = PX[:, :].rearrange("p (g c r) -> p g c r", g=G, c=4)

            def reciprocals(b, hf):
                dve.wait_ge(otr_done, 2 * b + hf + 1)
                nc.vector.reciprocal(RC[hf][:, :, :], by_head[:, :, :, D]).then_inc(rc_ready, 1)

            def normalise(b, hf, par, old):
                dve.wait_ge(rc_ready, 2 * b + hf + 1)
                if old:
                    dve.wait_ge(x1_ready, b)
                nc.vector.tensor_tensor(
                    AO[par][:, hf, :, :, :].rearrange("p c g d -> p g c d"), by_head[:, :, :, 0:D],
                    RC[hf][:, :, :].rearrange("p g (c o) -> p g c o", o=1).to_broadcast([128, G, 4, D]),
                    ALU.mult).then_inc(ao_ready, 1)

            def step(t, par, tt):
                nxt = 1 - par
                if tt == -2:
                    stacked_out(0, 0, 0, False)
                    statistics(2 * GB - 1)
                for c in range(NC):
                    if c == 2 and has(tt, 1) and tt != B - 2:
                        stacked_out(t + 1, 1, nxt, tt is None or tt >= 1)
                    if has(tt, 1):
                        maxima(t + 1, c, nxt)
                    if c == 0 and has(tt, 0):
                        shift_out(t, 1, tt == 0)
                    if c == 3 and has(tt, 1):
                        shift_high(t + 1, 0, nxt, tt == -1)
                    if c == 3 and has(tt, -1):
                        reciprocals(t - 1, 0)
                    if c == 3 and has(tt, 1):
                        shift_low(t + 1, 0, nxt)
                    if c == 4 and has(tt, -1):
                        normalise(t - 1, 0, nxt, tt is None or tt >= 3)
                    if c == 5 and has(tt, 1):
                        shift_out(t + 1, 0, tt == -1)
                    if c == 7 and has(tt, -1):
                        reciprocals(t - 1, 1)
                    if c == 7 and has(tt, 1):
                        shift_high(t + 1, 1, nxt, False)
                    if c == 7 and has(tt, -1):
                        normalise(t - 1, 1, nxt, False)
                    if c == 7 and has(tt, 1):
                        shift_low(t + 1, 1, nxt)
                    if tt == -1 and c == 0:
                        aggregates(2)
                    if tt in (-1, 0) and c < GB:
                        statistics(STAT[tt + 4].start + c)
                    if tt in (-1, 0) and c == GB:
                        aggregates(tt + 4)
                    if tt == 0 and c == 1:
                        keys_out(7)
                    if tt == 1 and c == 0:
                        signs_out(1)
                    if tt == B - 2:
                        if c < GB:
                            if c == 0:
                                dve.wait_ge(x1_ready, GB + 1)
                            norm_batch(0, c)
                        if c == GB:
                            dve.wait_ge(st2_ready, GB)
                            aggregate_group(0)
                        if c == 7:
                            apply_group(0)
                    if tt == B - 1:
                        if c == 0:
                            signs_out(2)
                        if c == 1:
                            low_group(0)
                        if c == 0:
                            output_factors()
                        if c == 3:
                            tokens_out(0, 0, True)
                        if c == 5:
                            signs_out(3)
                        if c == 6:
                            tokens_out(0, 1, True)
                    if tt == B and c in (5, 7):
                        hidden_low(0, (c - 5) // 2)
                if tt in (-1, 0, 1):
                    offsets(tt + 3)
                if tt == -1:
                    largest_scale()
            steps(dve, step)

            def group(n, first, more):
                for k in range(HK):
                    if more and k == 1:
                        dve.wait_ge(st2_ready, (n + 1) * GB + GB)
                    if not (first and k < 2):
                        hidden_low(n, k)
                    if more:
                        if k == 0:
                            norm_group(n + 1)
                        if k == 1:
                            aggregate_group(n + 1)
                        if k == 3:
                            apply_group(n + 1)
                        if k == 5:
                            low_group(n + 1)
                        if k >= 6:
                            tokens_out(n + 1, k - 6, False)
                if first:
                    dve.wait_ge(cs_ready, 1)
                for i in range(GB + 1):
                    if i < GB:
                        dve.wait_ge(y_done, n * GB + i + 1)
                        nc.vector.tensor_tensor(YS[:, i, :], YB[i][:, 0:E], CS[:, :], ALU.mult).then_inc(ys_ready, 1)
                    if i:
                        dve.wait_ge(ys_ready, n * GB + i)
                        xi = tokens_at(n, i - 1)
                        nc.vector.tensor_tensor(xi, xi, YS[:, i - 1, :], ALU.add).then_inc(y_ready, 1)

            group(0, True, True)
            with dve.Fori(1, NG - 1) as n:
                group(n, False, True)
            group(NG - 1, False, False)

        @block.tensor
        def _(pe):
            pe.wait_ge(ident, 2)

            def keys(i):
                pe.wait_ge(k_twice, 1 if i < GB // 2 else 2)
                if i >= 6:
                    keys_left(pe, i - 4)
                for a in range(2 * JP):
                    g0 = (2 * i * KVH) + 2 * a
                    last = nc.tensor.transpose(KBANK[i][:, a * 128:(a + 1) * 128],
                                               KP[:, g0:g0 + 2, :, :].rearrange("p j o c -> p (j o c)"), IDB[:, :])
                last.then_inc(k_tr, 1)

            def warm(bank, times):
                for i in range(times):
                    nc.tensor.transpose(bank[:, 0:128], IDF[:, :], IDF[:, :])

            keys(0)
            keys(1)
            warm(PX, 20)

            def stack(b, r):
                pe.wait_ge(lo_ready, b + 1)
                for a in range(2):
                    for g in range(G):
                        h0 = 2 * ((2 * r + a) * G + g)
                        last = nc.tensor.transpose(
                            PQh[:, (a * G + g) * 128:(a * G + g + 1) * 128],
                            QS[:, h0:h0 + 2, :, :].rearrange("p h c r -> p (h c r)"), IDH[:, :])
                last.then_inc(qtr_done, 1)

            def scores(b, c, par):
                rows = slice(64 * (c % 2), 64 * (c % 2) + 64)
                for g in range(G):
                    last = nc.tensor.matmul(PS_[c % 2][:, g * 128:(g + 1) * 128],
                                            QT[par][rows, c // 2, g * 128:(g + 1) * 128],
                                            KTS[par][rows, c // 2, :], start=True, stop=True)
                last.then_inc(s_done, 1)

            def shifted(b, c, par):
                rows = slice(64 * (c % 2), 64 * (c % 2) + 64)
                nc.tensor.matmul(PT_[c % 2][:, :], KTT[par][rows, c // 2, :], QT[par][rows, c // 2, :],
                                 start=True, stop=True).then_inc(t_done, 1)

            def sums(b, hf, par):
                for c in range(4):
                    last = nc.tensor.matmul(PO[32 * c:32 * c + 32, :], V[par][:, 4 * hf + c, :],
                                            P[par][:, 4 * hf + c, :], start=True, stop=True)
                last.then_inc(pv_done, 1)

            def queries_back(b, hf):
                pe.wait_ge(os_ready, 2 * b + hf + 1)
                for g in range(G):
                    last = nc.tensor.transpose(PX[:, g * 128:(g + 1) * 128], OS[hf][:, g * 128:(g + 1) * 128], IDF[:, :])
                last.then_inc(otr_done, 1)

            def shift_back(b, hf):
                pe.wait_ge(mp_ready, 2 * b + hf + 1)
                nc.tensor.transpose(PMh[0:32, 0:128], MP[:, :, :, :, :].rearrange("p a b c g -> p (a b c g)"),
                                    IDH[:, :]).then_inc(mtr_done, 1)

            def signs(i):
                pe.wait_ge(sign_done, 4 if i < FC else 8)
                for a in range(8):
                    if i < FC:
                        src = SU[:, a, i * 128:(i + 1) * 128]
                    else:
                        k, c = 4 * (i - FC) + a // FC, a % FC
                        src = SD[:, c, k * 128:(k + 1) * 128]
                    last = nc.tensor.transpose(SBANK[i][:, a * 128:(a + 1) * 128], src, IDH[:, :])
                last.then_inc(wtr_done, 1)

            def tokens(n, p, first):
                if p == 0:
                    pe.wait_ge(xh_ready, n + 1)
                    if first:
                        pe.wait_ge(wt_dve, 2)
                    else:
                        pe.wait_ge(xt_ready, 2 * n)
                else:
                    pe.wait_ge(xl_ready, n + 1)
                    pe.wait_ge(xt_ready, 2 * n + 1)
                for c in range(FC):
                    for i in range(GB):
                        a = c * GB + i
                        last = nc.tensor.transpose(PQh[:, a * 128:(a + 1) * 128],
                                                   XH[:, p, i, c * 128:(c + 1) * 128], IDH[:, :])
                last.then_inc(xtr_done, 1)

            def up(n, k, first):
                if k == 0:
                    pe.wait_ge(xt_ready, 2 * n + 2)
                    if first:
                        pe.wait_ge(mt_ready, 2 * B)
                        pe.wait_ge(wt_dve, 3)
                if k >= 3:
                    pe.wait_ge(hh_ready, n * HK + k - 2)
                elif not first:
                    pe.wait_ge(hh_ready, n * HK + (-1, 0, -2)[k])
                for p in range(2):
                    for c in range(FC):
                        last = nc.tensor.matmul(UPB[k % 3][:, :], UT[:, c, k * 128:(k + 1) * 128], XT[:, p, c, :],
                                                start=(p == 0 and c == 0), stop=(p == 1 and c == FC - 1))
                last.then_inc(up_done, 1)

            K_AT = {0: 3, 1: 4, 3: 5, 5: 6, 6: 7}

            def step(t, par, tt):
                nxt = 1 - par
                if has(tt, 1):
                    pe.wait_ge(kts_ld[nxt], 16 * turn(t, par, 1))
                    pe.wait_ge(qt_ready[0], t + 2)
                    if tt != -1:
                        pe.wait_ge(max_done, NC * (t + 1) - 1)
                    scores(t + 1, 0, nxt)
                for c in range(NC):
                    if has(tt, 1) and c + 1 < NC:
                        if c + 1 == 4:
                            pe.wait_ge(qt_ready[1], t + 2)
                        if tt != -1 or c >= 1:
                            pe.wait_ge(max_done, NC * (t + 1) + c)
                        scores(t + 1, c + 1, nxt)
                    if has(tt, 0):
                        if c == 0:
                            pe.wait_ge(ktt_ld[par], 16 * turn(t, par, 0))
                            pe.wait_ge(m_ld[0], 16 * (t + 1))
                        if c == 4:
                            pe.wait_ge(m_ld[1], 16 * (t + 1))
                        if tt != 0 or c >= 2:
                            pe.wait_ge(exp_done, NC * t + c - 1)
                        else:
                            keys_left(pe, 4 + c)
                        shifted(t, c, par)
                    if c == 0 and has(tt, 0):
                        pe.wait_ge(mt_ready, 2 * t + 1)
                        shift_back(t, 1)
                    if c == 0 and has(tt, 1):
                        pe.wait_ge(qt_ready[0], t + 2)
                        stack(t + 1, 1)
                    if c == 2 and has(tt, -1):
                        if tt != 1:
                            pe.wait_ge(ao_ready, 2 * t - 2)
                        else:
                            pe.wait_ge(wt_dve, 1)
                        queries_back(t - 1, 0)
                    if c == 1:
                        if has(tt, -1):
                            pe.wait_ge(exp_done, NC * t)
                            pe.wait_ge(os_ready, 2 * t - 1)
                            sums(t - 1, 1, nxt)
                    if c == 6 and has(tt, -1):
                        pe.wait_ge(ao_ready, 2 * t - 1)
                        queries_back(t - 1, 1)
                    if c == 5 and has(tt, 0):
                        pe.wait_ge(v_ld[par], 16 * turn(t, par, 0))
                        pe.wait_ge(exp_done, NC * t + 4)
                        if tt != 0:
                            pe.wait_ge(os_ready, 2 * t)
                        else:
                            pe.wait_ge(wt_act, 1)
                        sums(t, 0, par)
                    if c == 4 and has(tt, 1):
                        if tt == -1:
                            keys_left(pe, 1)
                        else:
                            pe.wait_ge(mt_ready, 2 * (t + 1))
                        shift_back(t + 1, 0)
                    if tt == -2 and c == 4:
                        keys(2)
                    if c == 4 and has(tt, 2):
                        if tt == -2:
                            keys_left(pe, 0)
                        else:
                            pe.wait_ge(qt_ready[1], t + 2)
                        stack(t + 2, 0)
                    if tt == -1 and c in K_AT:
                        keys(K_AT[c])
                    if tt == -1 and c < 3:
                        keys_left(pe, 1)
                        warm(PM, (2, 2, 2)[c])
                    if tt == 0 and c == 1:
                        keys_left(pe, 6)
                        signs(0)
                    if tt == 0 and c == 3:
                        keys_left(pe, 7)
                        signs(1)
                    if tt == B - 2 and c == 6:
                        signs(2)
                    if tt == B - 1:
                        if c == 1:
                            pe.wait_ge(max_done, NC * B)
                            signs(3)
                        if c == 3:
                            tokens(0, 0, True)
                        if c == 5:
                            tokens(0, 1, True)
                        if c == 7:
                            up(0, 0, True)
                    if tt == B and c == 2:
                        up(0, 1, True)
                    if tt == B and c == 6:
                        up(0, 2, True)
            steps(pe, step)

            def down(n, k, first):
                pe.wait_ge(hl_ready, n * HK + k + 1)
                for i in range(GB):
                    if k == 0:
                        if not first:
                            pe.wait_ge(ys_ready, n * GB + i - GB + 1)
                        elif i == 0:
                            pe.wait_ge(exp_done, NC * B)
                        elif i == 2:
                            pe.wait_ge(os_ready, 2 * B)
                        elif i == 3:
                            pe.wait_ge(ao_ready, 2 * B)
                    for p in range(2):
                        last = nc.tensor.matmul(YB[i][:, 0:E], HP[k % 4][:, p, i * 128:(i + 1) * 128], DT[:, k, :],
                                                start=(k == 0 and p == 0), stop=(k == HK - 1 and p == 1))
                    if k == HK - 1:
                        last.then_inc(y_done, 1)
                if k < HK - 1:
                    last.then_inc(down_done, 1)

            def group(n, first, more):
                for k in range(HK + 2):
                    if k < HK and not (first and k < 3):
                        up(n, k, first)
                    if k >= 2:
                        if more and k >= HK:
                            tokens(n + 1, k - HK, False)
                        down(n, k - 2, first)

            group(0, True, True)
            with pe.Fori(1, NG - 1) as n:
                group(n, False, True)
            group(NG - 1, False, False)


_INS = ['x', 'ctx_512', 'g_xattn', 'g_ffn', 'L0_ffn_up_weight', 'L0_ffn_down_weight', 'L0_ffn_up_scale',
        'L0_ffn_down_scale', 'L0_ffn_output_scale']


def kernel(**inputs):
    import numpy as _np
    import concourse.bacc as _bacc
    from concourse import mybir as _mybir
    from concourse.bass_utils import run_bass_kernel_spmd as _run

    nc = _bacc.Bacc("TRN2", target_bir_lowering=False, num_devices=1)
    arrays, args = {}, []
    for name in _INS:
        a = _np.ascontiguousarray(inputs[name])
        arrays[f"in_{name}"] = a
        args.append(nc.dram_tensor(f"in_{name}", a.shape, _mybir.dt.from_np(a.dtype), kind="ExternalInput").ap())
    args.append(nc.dram_tensor("out_0", inputs['x'].shape, _mybir.dt.float32, kind="ExternalOutput").ap())
    flamingo_kernel(nc, *args)
    r = _run(nc, [arrays], core_ids=[0])
    return r.results[0]["out_0"]
```
